# Optimizing a Trainium2 kernel written in Bass

```python
import numpy as np
import jax
import jax.numpy as jnp

def _softmax(x, axis=-1):
    return jax.nn.softmax(x, axis=axis)

def _gelu(x):
    return jax.nn.gelu(x, approximate=True)

def _silu(x):
    return jax.nn.silu(x)

def _sigmoid(x):
    return jax.nn.sigmoid(x)

def _layernorm(x, axis=-1, eps=1e-05):
    m = jnp.mean(x, axis=axis, keepdims=True)
    v = jnp.var(x, axis=axis, keepdims=True)
    return (x - m) / jnp.sqrt(v + eps)

def _scatter_add(tgt, idx, src, axis=0):
    return tgt.at[idx].add(src)

def _segment_sum(src, seg, n):
    return jax.ops.segment_sum(src, seg, n)
kernel_name = 'mk_prb_d1_jaxref_r8_894094'

def setup_inputs(seed: int=0):
    np.random.seed(seed)
    _w = jnp.asarray

    def _L0_attn_setup():
        import jax, jax.numpy as jnp
        import numpy as np
        B, S, E, H, Dh = (2, 256, 128, 16, 64)
        key = jax.random.key(seed)
        ks = jax.random.split(key, 8)
        w = 0.02
        return {'x': jax.random.normal(ks[0], (B, S, E), jnp.float32), 'Wq': jax.random.normal(ks[1], (H, Dh, E), jnp.float32) * w, 'bq': jax.random.normal(ks[2], (H, Dh), jnp.float32) * w, 'Wk': jax.random.normal(ks[3], (H, Dh, E), jnp.float32) * w, 'bk': jax.random.normal(ks[4], (H, Dh), jnp.float32) * w, 'Wv': jax.random.normal(ks[5], (H, Dh, E), jnp.float32) * w, 'bv': jax.random.normal(ks[6], (H, Dh), jnp.float32) * w, 'proj': jax.random.normal(ks[7], (H * Dh, E), jnp.float32) * w}
    _L0_attn_in = _L0_attn_setup()

    def _L0_ffn_setup():
        import jax, jax.numpy as jnp
        import numpy as np
        B, C, D, O = (4, 512, 128, 128)
        PROJ = 32
        RANKS = [1, 2, 4, 8]
        E = len(RANKS)
        CLAMP_MAX = float(np.log(1.0 / 0.01))

        def _l2norm(v, axis):
            return v / jnp.maximum(jnp.linalg.norm(v, axis=axis, keepdims=True), 1e-12)
        key = jax.random.key(seed)
        ks = jax.random.split(key, 16)
        inp = {'x': jax.random.normal(ks[0], (B, C, D), dtype=jnp.float32), 'W': jax.random.normal(ks[1], (O, D), dtype=jnp.float32) / np.sqrt(D), 'Wp': jax.random.normal(ks[2], (PROJ, D), dtype=jnp.float32) / np.sqrt(D), 'bp': jnp.zeros((PROJ,), dtype=jnp.float32), 'sim': jax.random.normal(ks[3], (PROJ, E), dtype=jnp.float32) * 0.01, 'temp': jnp.full((1,), np.log(1.0 / 0.5), dtype=jnp.float32)}
        for i, r in enumerate(RANKS):
            inp[f'Wd{i}'] = jax.random.normal(ks[4 + 2 * i], (r, D), dtype=jnp.float32) / r
            inp[f'Wu{i}'] = jax.random.normal(ks[5 + 2 * i], (O, r), dtype=jnp.float32) * 0.01
        return inp
    _L0_ffn_in = _L0_ffn_setup()
    _d = {'L0_attn_x': _L0_attn_in['x'], 'L0_attn_Wq': _L0_attn_in['Wq'], 'L0_attn_bq': _L0_attn_in['bq'], 'L0_attn_Wk': _L0_attn_in['Wk'], 'L0_attn_bk': _L0_attn_in['bk'], 'L0_attn_Wv': _L0_attn_in['Wv'], 'L0_attn_bv': _L0_attn_in['bv'], 'L0_attn_proj': _L0_attn_in['proj'], 'L0_ffn_W': _L0_ffn_in['W'], 'L0_ffn_Wp': _L0_ffn_in['Wp'], 'L0_ffn_bp': _L0_ffn_in['bp'], 'L0_ffn_sim': _L0_ffn_in['sim'], 'L0_ffn_temp': _L0_ffn_in['temp'], 'L0_ffn_Wd0': _L0_ffn_in['Wd0'], 'L0_ffn_Wu0': _L0_ffn_in['Wu0'], 'L0_ffn_Wd1': _L0_ffn_in['Wd1'], 'L0_ffn_Wu1': _L0_ffn_in['Wu1'], 'L0_ffn_Wd2': _L0_ffn_in['Wd2'], 'L0_ffn_Wu2': _L0_ffn_in['Wu2'], 'L0_ffn_Wd3': _L0_ffn_in['Wd3'], 'L0_ffn_Wu3': _L0_ffn_in['Wu3']}
    _x0 = _d['L0_attn_x']
    _d['L0_attn_x'] = jax.random.normal(jax.random.fold_in(jax.random.key(seed), 1), (16, 512, 128), dtype=_x0.dtype)
    del _x0
    return _d

def reference(L0_attn_x, L0_attn_Wq, L0_attn_bq, L0_attn_Wk, L0_attn_bk, L0_attn_Wv, L0_attn_bv, L0_attn_proj, L0_ffn_W, L0_ffn_Wp, L0_ffn_bp, L0_ffn_sim, L0_ffn_temp, L0_ffn_Wd0, L0_ffn_Wu0, L0_ffn_Wd1, L0_ffn_Wu1, L0_ffn_Wd2, L0_ffn_Wu2, L0_ffn_Wd3, L0_ffn_Wu3):

    def _L0_attn_ref(x, Wq, bq, Wk, bk, Wv, bv, proj):
        import jax, jax.numpy as jnp
        import numpy as np
        B, S, E, H, Dh = (2, 256, 128, 16, 64)
        b, s, e = x.shape
        h, dh, _ = Wq.shape
        scale = jnp.sqrt(jnp.asarray(dh, x.dtype))
        q = jnp.einsum('bse,hde->bhsd', x, Wq) + bq[None, :, None, :]
        k = jnp.einsum('bse,hde->bhsd', x, Wk) + bk[None, :, None, :]
        v = jnp.einsum('bse,hde->bhsd', x, Wv) + bv[None, :, None, :]
        causal = jnp.triu(jnp.ones((s, s), bool), 1)
        scores = jnp.einsum('bhsd,bhtd->bhst', q, k) / scale
        scores = jnp.where(causal[None, None], -jnp.inf, scores)
        att = jax.nn.softmax(scores, axis=-1) / scale
        z = jnp.einsum('bhst,bhtd->bhsd', att, v)
        z = z.reshape(b, s, h * dh)
        return z @ proj

    def _L0_ffn_ref(x, W, Wp, bp, sim, temp, Wd0, Wu0, Wd1, Wu1, Wd2, Wu2, Wd3, Wu3):
        import jax, jax.numpy as jnp
        import numpy as np
        B, C, D, O = (4, 512, 128, 128)
        PROJ = 32
        RANKS = [1, 2, 4, 8]
        E = len(RANKS)
        CLAMP_MAX = float(np.log(1.0 / 0.01))

        def _l2norm(v, axis):
            return v / jnp.maximum(jnp.linalg.norm(v, axis=axis, keepdims=True), 1e-12)
        base = jnp.einsum('bcd,od->bco', x, W)
        xf = x.reshape(-1, x.shape[-1])
        proj = _l2norm(xf @ Wp.T + bp, axis=1)
        simn = _l2norm(sim, axis=0)
        scale = jnp.exp(jnp.minimum(temp, CLAMP_MAX))
        logits = proj @ simn * scale
        lw = jax.nn.softmax(logits, axis=1)
        top1 = jnp.argmax(lw, axis=1)
        ret = jnp.where(jnp.arange(E)[None, :] == top1[:, None], lw, 0.0)
        ret = ret.reshape(x.shape[0], x.shape[1], E)
        downs = (Wd0, Wd1, Wd2, Wd3)
        ups = (Wu0, Wu1, Wu2, Wu3)
        l = jnp.stack([jnp.einsum('bcr,or->bco', jnp.einsum('bcd,rd->bcr', x, d), u) for d, u in zip(downs, ups)], axis=2)
        res = jnp.sum(ret[..., None] * l, axis=2)
        return base + res
    x = L0_attn_x
    xn = _layernorm(x, axis=-1)
    x = x + _L0_attn_ref(xn, L0_attn_Wq, L0_attn_bq, L0_attn_Wk, L0_attn_bk, L0_attn_Wv, L0_attn_bv, L0_attn_proj) + _L0_ffn_ref(xn, L0_ffn_W, L0_ffn_Wp, L0_ffn_bp, L0_ffn_sim, L0_ffn_temp, L0_ffn_Wd0, L0_ffn_Wu0, L0_ffn_Wd1, L0_ffn_Wu1, L0_ffn_Wd2, L0_ffn_Wu2, L0_ffn_Wd3, L0_ffn_Wu3)
    return x

_drawn_inputs = setup_inputs


def setup_inputs(seed=0):
    import zlib

    import numpy as np

    out = dict(_drawn_inputs(seed))
    spreads = {'L0_ffn_bp': (0.0, 0.8)}
    factors = {'L0_attn_Wq': 8.0,
     'L0_attn_bq': 8.0,
     'L0_attn_Wk': 8.0,
     'L0_attn_bk': 8.0,
     'L0_attn_Wv': 8.0,
     'L0_attn_bv': 8.0,
     'L0_attn_proj': 8.0,
     'L0_ffn_Wp': 3.079,
     'L0_ffn_sim': 2.981,
     'L0_ffn_Wd0': 3.469,
     'L0_ffn_Wu0': 3.253,
     'L0_ffn_Wd1': 5.642,
     'L0_ffn_Wu1': 5.608,
     'L0_ffn_Wd2': 7.971,
     'L0_ffn_Wu2': 7.913,
     'L0_ffn_Wd3': 8.0,
     'L0_ffn_Wu3': 8.0}
    for name, (base, spread) in spreads.items():
        noise = np.random.default_rng([zlib.crc32(name.encode()), seed]).standard_normal(out[name].shape)
        drawn = base * np.exp(spread * noise) if base else spread * noise
        out[name] = jnp.asarray(drawn.astype(out[name].dtype))
    for name, factor in factors.items():
        out[name] = (out[name] * factor).astype(out[name].dtype)
    return out
```

```python
from contextlib import ExitStack

import concourse.bass as bass
from concourse import mybir

F32 = mybir.dt.float32
F32R = mybir.dt.float32r
ALU = mybir.AluOpType
ACT = mybir.ActivationFunctionType
AX_X = mybir.AxisListType.X

P = 128
NBATCH, S, E = 16, 512, 128
H, DH = 16, 64
NPAIR = H // 2
NBLK = S // P
RANKS = (1, 2, 4, 8)
NEXP = len(RANKS)
RSUM = sum(RANKS)
PROJ = 32
NRD = PROJ + RSUM
RPAD = 48
LN_EPS = 1e-5
CLAMP_MAX = 4.605170185988092
L2_EPS = 1e-12
INV_SCALE = 1.0 / DH ** 0.5
MASKED = -1e30
HUGE = 3e38

UNITS = NPAIR * NBLK
LAG_T = 3
LAG_PV = 7
LAG_Z = 8
QUAD = 4
NQUAD = H // QUAD
ROWS = S // H
LAG_OUT = 12
NROT = 4

JOBS = {}
for _p in range(NPAIR):
    JOBS[NBLK * _p] = ("q", (_p + 1) % NPAIR)
    JOBS[NBLK * _p + 1] = ("k", (_p + 1) % NPAIR)
JOBS[14] = ("router", 0)
JOBS[26] = ("xt", 0)
JOBS[27] = ("gated", 0)
V_STEPS = (30, 31, 2, 3, 6, 7, 10, 11)
for _n, _s in enumerate(V_STEPS):
    JOBS[_s] = ("v", _n)
AHEAD = (26, 28, 29, 30, 31)
HI_KINDS = ("q", "k", "xt")

STEP_ROUTER, STEP_GATED = 14, 27
STEP_FINAL, STEP_BASE, STEP_LORA = 5, 6, 30
STEP_STATS, STEP_NORM = 20, 24
R_CHAIN = 20


def bank_of(s):
    return s % 2


def count_jobs(s, kinds=None):
    jobs = [j for j in JOBS if bank_of(j) == bank_of(s) and (kinds is None or JOBS[j][0] in kinds)]
    return len([j for j in jobs if j in AHEAD]) + len([j for j in jobs if j <= s]), len(jobs)


class Counts:

    def __init__(self, eng, b):
        self.eng, self.b, self.base = eng, b, {}

    def at(self, per_batch, k):
        if isinstance(self.b, int):
            return self.b * per_batch + k
        if per_batch not in self.base:
            self.base[per_batch] = self.eng.snap(self.b * per_batch)
        return self.base[per_batch] + k if k else self.base[per_batch]

    def fixed(self, value):
        if not isinstance(value, int):
            self.eng.compute_val(value)
        return value

    def head(self, s, h):
        return self.at(2 * UNITS, 2 * s + h + 1)

    def unit(self, s):
        return self.at(UNITS, s + 1)

    def pair(self, p):
        return self.at(NPAIR, p + 1)

    def quad(self, g):
        return self.at(NQUAD, g + 1)

    def job(self, s, back=0):
        n, per_batch = count_jobs(s)
        return self.at(per_batch, n - back * per_batch)

    def hi(self, s):
        n, per_batch = count_jobs(s, HI_KINDS)
        return self.at(per_batch, n)


def wait(eng, semaphore, value):
    if not isinstance(value, int) or value > 0:
        eng.wait_ge(semaphore, value)


def width(s):
    return P * (s % NBLK + 1)


def build(nc, x, Wq, bq, Wk, bk, Wv, bv, proj, W, Wp, bp, sim, temp, Wd, Wu, out):
    with ExitStack() as ctx:
        def sb(name, shape, dt=F32):
            return ctx.enter_context(nc.sbuf_tensor(name, shape, dt))

        def psum(name):
            return ctx.enter_context(nc.psum_tensor(name, [P, S], F32))

        def sem(name):
            return ctx.enter_context(nc.semaphore(name))

        scores = [psum(f"scores{h}") for h in range(2)]
        ptp = [psum(f"ptp{h}") for h in range(2)]
        zp = psum("zp")
        outp = psum("outp")
        jobp = [psum(f"jobp{n}") for n in range(2)]
        weight_banks = [*scores, *ptp, zp, outp]

        w_in = [sb(f"w_in{n}", [P, NPAIR, E]) for n in range(3)]
        w_hi = [sb(f"w_hi{n}", [P, H * DH], F32R) for n in range(3)]
        w_lo = [sb(f"w_lo{n}", [P, H * DH], F32R) for n in range(3)]
        projs = sb("projs", [P, NPAIR, E])
        small_in = sb("small_in", [P, 4, P])
        wt = sb("wt", [P, E])
        wrd = sb("wrd", [P, NRD])
        wut = sb("wut", [RSUM, E])
        bqk = sb("bqk", [P, 2 * NPAIR])
        bv_b = sb("bv_b", [P, H * DH])
        bv8 = sb("bv8", [P, H * DH])
        bp_b = sb("bp_b", [P, PROJ])
        sim_b = sb("sim_b", [P, PROJ, NEXP])
        sim_sq = sb("sim_sq", [P, PROJ, NEXP])
        sim_unit = sb("sim_unit", [P, NEXP, PROJ])
        simn = sb("simn", [P, NEXP, PROJ])
        sim_norm = sb("sim_norm", [P, 4, NEXP])
        temp_b = sb("temp_b", [P, 1])
        temp_c = sb("temp_c", [P, 1])
        gate_scale = sb("gate_scale", [P, 1])
        ident = sb("ident", [P, P])
        mask = sb("mask", [P, S])
        power = sb("power", [P, 2, NBLK])

        xin = sb("xin", [P, NBLK, E])
        stats = sb("stats", [P, NBLK, 6])
        meanvar = sb("meanvar", [P, NBLK, 2])
        eps = sb("eps", [P, NBLK])
        var_eps = sb("var_eps", [P, NBLK])
        rstd = sb("rstd", [P, NBLK])
        xn = sb("xn", [P, NBLK, E])
        xt = sb("xt", [P, S])
        xt_hi = sb("xt_hi", [P, S], F32R)
        xt_lo = sb("xt_lo", [P, S], F32R)
        xres = sb("xres", [P, NBLK, E])
        osb = sb("osb", [P, NBLK, E])

        q_hi = sb("q_hi", [P, 2, S], F32R)
        q_lo = sb("q_lo", [P, 2, S], F32R)
        k_hi = sb("k_hi", [P, 2, S], F32R)
        k_lo = sb("k_lo", [P, 2, S], F32R)
        v_sb = sb("v_sb", [P, NBLK, H * DH])
        sm = sb("sm", [P, 2, 2, S])
        nmax = sb("nmax", [P, NROT, 2])
        den = sb("den", [P, NROT, 2])
        rden = sb("rden", [P, NROT, 2])
        prob = sb("prob", [P, NROT, 2, S])
        pt = sb("pt", [P, 2, 2, NBLK, S])
        zs = sb("zs", [P, 2, QUAD, NPAIR, ROWS])

        u = sb("u", [P, NBLK, PROJ])
        dn = sb("dn", [P, NBLK, RSUM])
        usq = sb("usq", [P, NBLK, PROJ])
        unorm = sb("unorm", [P, 4, NBLK])
        uprod = sb("uprod", [P, NBLK, NEXP, PROJ])
        lg = sb("lg", [P, 7, NBLK, NEXP])
        row = sb("row", [P, 5, NBLK])
        gated = sb("gated", [P, NBLK, RSUM])
        gated_t = sb("gated_t", [RSUM, S])

        w_loaded = [sem(f"w_loaded{n}") for n in range(3)]
        small_loaded = sem("small_loaded")
        xin_loaded = sem("xin_loaded")
        xres_loaded = sem("xres_loaded")
        out_stored = sem("out_stored")
        zeroed = sem("zeroed")
        consts_ready = sem("consts_ready")
        wbank_ready = sem("wbank_ready")
        w_hi_ready = sem("w_hi_ready")
        w_lo_ready = sem("w_lo_ready")
        small_bank_ready = sem("small_bank_ready")
        small_ready = sem("small_ready")
        setup_chain = sem("setup_chain")
        simsq_ready = sem("simsq_ready")
        simnorm_ready = sem("simnorm_ready")
        temp_ready = sem("temp_ready")
        gate_scale_ready = sem("gate_scale_ready")
        ln_chain = sem("ln_chain")
        var_ready = sem("var_ready")
        rstd_ready = sem("rstd_ready")
        xn_ready = sem("xn_ready")
        s_ready = sem("s_ready")
        sm_ready = sem("sm_ready")
        p_ready = sem("p_ready")
        r_ready = sem("r_ready")
        pn_ready = sem("pn_ready")
        t_ready = sem("t_ready")
        pt_ready = [sem(f"pt_ready{h}") for h in range(2)]
        pv_ready = sem("pv_ready")
        z_ready = sem("z_ready")
        o_ready = sem("o_ready")
        final_ready = sem("final_ready")
        job_ready = [sem(f"job_ready{n}") for n in range(2)]
        job_hi = [sem(f"job_hi{n}") for n in range(2)]
        job_done = [sem(f"job_done{n}") for n in range(2)]
        unorm_ready = sem("unorm_ready")
        unorm_root = sem("unorm_root")
        lg_ready = sem("lg_ready")
        lg_exp = sem("lg_exp")
        gated_ready = sem("gated_ready")
        r_chain = sem("r_chain")

        block = ctx.enter_context(nc.Block())
        n_small = 2 + 2 * NEXP + 7

        @block.sync
        def _(sp):
            def tok(t):
                return t.rearrange("(n p) e -> p n e", p=P)

            sp.dma_start(xin[:], tok(x[0])).then_inc(xin_loaded, 16)
            for n, w in enumerate((Wq, Wk, Wv)):
                sp.dma_start(w_in[n][:], w.rearrange("(c a) d e -> (a d) c e", a=2)).then_inc(w_loaded[n], 16)
            sp.dma_start(small_in[:, 0, :], W).then_inc(small_loaded, 16)
            sp.dma_start(small_in[0:PROJ, 1, :], Wp).then_inc(small_loaded, 16)
            r0 = 0
            for n, r in enumerate(RANKS):
                sp.dma_start(small_in[PROJ + r0:PROJ + r0 + r, 1, :], Wd[n]).then_inc(small_loaded, 16)
                sp.dma_start(small_in[:, 2, r0:r0 + r], Wu[n]).then_inc(small_loaded, 16)
                r0 += r
            for n, t in enumerate((bq, bk)):
                sp.dma_start(small_in[NPAIR * n:NPAIR * (n + 1), 3, :],
                             t.rearrange("(c a) d -> c (a d)", a=2)).then_inc(small_loaded, 16)
            sp.dma_start(bv_b[:], bv.rearrange("h d -> (h d)").partition_broadcast(P)).then_inc(small_loaded, 16)
            sp.dma_start(bp_b[:], bp.partition_broadcast(P)).then_inc(small_loaded, 16)
            sp.dma_start(sim_b[:].rearrange("p a b -> p (a b)"),
                         sim.rearrange("a b -> (a b)").partition_broadcast(P)).then_inc(small_loaded, 16)
            sp.dma_start(temp_b[:], temp.partition_broadcast(P)).then_inc(small_loaded, 16)
            sp.dma_start(projs[:], proj.rearrange("(c p) e -> p c e", p=P)).then_inc(small_loaded, 16)

            def rows(t, b):
                if isinstance(b, int):
                    return tok(t[b])
                return t[bass.ds(b, 1), :, :].rearrange("o (n p) e -> p (o n) e", p=P)

            def batch(b):
                c = Counts(sp, b)
                first, last = b == 0 if isinstance(b, int) else False, b is last_batch
                if not last:
                    sp.wait_ge(xn_ready, c.at(1, 1))
                    sp.dma_start(xin[:], rows(x, b + 1)).then_inc(xin_loaded, 16)
                if not first:
                    sp.wait_ge(final_ready, c.at(1, 0))
                    sp.dma_start(rows(out, b - 1), osb[:]).then_inc(out_stored, 16)
                    sp.wait_ge(out_stored, c.at(16, 0))
                sp.dma_start(xres[:], rows(x, b)).then_inc(xres_loaded, 16)

            last_batch = NBATCH - 1
            batch(0)
            with sp.Fori(1, last_batch) as b:
                batch(b)
            batch(last_batch)
            sp.wait_ge(final_ready, NBATCH)
            sp.dma_start(tok(out[last_batch]), osb[:]).then_inc(out_stored, 16)
            sp.wait_ge(out_stored, 16 * NBATCH)

        @block.gpsimd
        def _(pool):
            nc.gpsimd.memset(ident[:], 0.0).then_inc(zeroed, 1)
            nc.gpsimd.memset(mask[:], 0.0).then_inc(zeroed, 1)
            nc.gpsimd.memset(power[:, 0, :], -0.5).then_inc(zeroed, 1)
            nc.gpsimd.memset(power[:, 1, :], 0.5).then_inc(zeroed, 1)
            pool.wait_ge(zeroed, 4)
            nc.gpsimd.affine_select(out=ident[:], in_=ident[:], compare_op=ALU.not_equal, fill=1.0,
                                    base=0, pattern=[[-1, P]], channel_multiplier=1).then_inc(consts_ready, 1)
            for odd in range(2):
                pool.wait_ge(consts_ready, 1 + odd)
                diagonal = mask[64 * odd:64 * odd + 64, S - P:S]
                nc.gpsimd.affine_select(out=diagonal, in_=diagonal, compare_op=ALU.is_ge, fill=MASKED,
                                        base=odd, pattern=[[-1, P]], channel_multiplier=2).then_inc(consts_ready, 1)

            def root(c):
                pool.wait_ge(var_ready, c.at(1, 2))
                nc.gpsimd.tensor_tensor(rstd[:], var_eps[:], power[:, 0, :], ALU.pow).then_inc(rstd_ready, 1)

            pool.wait_ge(consts_ready, 3)
            root(Counts(pool, -1))
            pool.wait_ge(simsq_ready, 1)
            nc.gpsimd.tensor_tensor(sim_norm[:, 1, :], sim_norm[:, 0, :], power[:, 1, 0:NEXP], ALU.pow)\
                .then_inc(simnorm_ready, 1)

            def normalise(c, s):
                pool.wait_ge(r_ready, c.unit(s))
                for h in range(2):
                    part = prob[:, s % NROT, h, 0:width(s)]
                    scale = rden[:, s % NROT, h:h + 1].to_broadcast([P, width(s)])
                    nc.gpsimd.tensor_tensor(part, part, scale, ALU.mult).then_inc(pn_ready, 1)

            def batch(b, last):
                c = Counts(pool, b)
                for s in range(UNITS):
                    if s == STEP_ROUTER + 3:
                        pool.wait_ge(unorm_ready, c.at(1, 1))
                        nc.gpsimd.tensor_tensor(unorm[:, 1, :], unorm[:, 0, :], power[:, 1, :], ALU.pow)\
                            .then_inc(unorm_root, 1)
                    if s == STEP_STATS + 2 and not last:
                        root(c)
                    normalise(c, s)

            batch(0, False)
            with pool.Fori(1, NBATCH - 1) as b:
                batch(b, False)
            batch(NBATCH - 1, True)

        @block.scalar
        def _(act):
            for n, bank in enumerate(weight_banks):
                act.wait_ge(wbank_ready, n + 1)
                nc.scalar.activation(w_hi[n // 2][:, S * (n % 2):S * (n % 2) + S], bank[:], ACT.Copy)\
                    .then_inc(w_hi_ready, 1)
            act.wait_ge(temp_ready, 1)
            nc.scalar.activation(gate_scale[:], temp_c[:], ACT.Exp).then_inc(gate_scale_ready, 1)

            def job(c, s):
                kind, n = JOBS[s]
                bank = bank_of(s)
                if kind not in HI_KINDS:
                    return
                act.wait_ge(job_ready[bank], c.job(s))
                if kind == "xt":
                    nc.scalar.activation(xt_hi[:], jobp[bank][:], ACT.Copy)
                    nc.scalar.activation(xt[:], jobp[bank][:], ACT.Copy).then_inc(job_hi[bank], 1)
                else:
                    dst, col = (q_hi, n) if kind == "q" else (k_hi, NPAIR + n)
                    nc.scalar.activation(dst[:, n % 2, :], jobp[bank][:], ACT.Identity, bias=bqk[:, col:col + 1])\
                        .then_inc(job_hi[bank], 1)

            def evacuate_z(c, p):
                act.wait_ge(pv_ready, c.pair(p))
                if p % 2 == 0:
                    wait(act, o_ready, c.quad(p // 2 - 2))
                src = zp[:].rearrange("p (h r c) -> p h c r", h=2, c=NPAIR)
                dst = zs[:, p // 2 % 2, 2 * (p % 2):2 * (p % 2) + 2, :, :]
                nc.scalar.activation(dst, src, ACT.Copy).then_inc(z_ready, 1)

            def exponentials(c, s):
                for h in range(2):
                    act.wait_ge(sm_ready, c.head(s, h))
                    wait(act, t_ready, c.head(s - NROT, h))
                    nc.scalar.activation(prob[:, s % NROT, h, 0:width(s)], sm[:, s % 2, h, 0:width(s)], ACT.Exp,
                                         bias=nmax[:, s % NROT, h:h + 1], scale=-1.0,
                                         accum_out=den[:, s % NROT, h:h + 1]).then_inc(p_ready, 1)

            def evacuate_pt(c, s):
                act.wait_ge(t_ready, c.head(s, 0))
                i, p = s % NBLK, s // NBLK
                if i == 0:
                    wait(act, pv_ready, c.pair(p - 2))
                src = ptp[0][:, 0:width(s)].rearrange("p (j q) -> p j q", q=P)
                nc.scalar.activation(pt[:, p % 2, 0, 0:i + 1, P * i:P * i + P], src, ACT.Copy)\
                    .then_inc(pt_ready[0], 1)

            act.wait_ge(small_ready, 4)
            for s in AHEAD:
                job(Counts(act, -1), s)

            def batch(b, first, last):
                c = Counts(act, b)
                for s in range(UNITS):
                    if s % NBLK == LAG_Z % NBLK and (s >= LAG_Z or not first):
                        evacuate_z(c, (s - LAG_Z) // NBLK)
                    if s - 1 in JOBS and not (last and s - 1 in AHEAD):
                        job(c, s - 1)
                    if s == STEP_ROUTER + 5:
                        act.wait_ge(lg_ready, c.at(1, 1))
                        nc.scalar.activation(lg[:, 3, :, :], lg[:, 2, :, :], ACT.Exp).then_inc(lg_exp, 1)
                    exponentials(c, s)
                    if s >= LAG_T or not first:
                        evacuate_pt(c, s - LAG_T)

            batch(0, True, False)
            with act.Fori(1, NBATCH - 1) as b:
                batch(b, False, False)
            batch(NBATCH - 1, False, True)
            c = Counts(act, NBATCH)
            for s in range(STEP_FINAL):
                if s % NBLK == LAG_Z % NBLK:
                    evacuate_z(c, (s - LAG_Z) // NBLK)
                if s < LAG_T:
                    evacuate_pt(c, s - LAG_T)

        @block.vector
        def _(dve):
            def statistics(c):
                dve.wait_ge(xin_loaded, c.at(16, 32))
                for n in range(NBLK):
                    last = nc.vector.bn_stats(stats[:, n, :], xin[:, n, :])
                last.then_inc(ln_chain, 1)
                dve.wait_ge(ln_chain, c.at(2, 3))
                nc.vector.memset(eps[:], LN_EPS)
                for n in range(NBLK):
                    last = nc.vector.bn_aggr(meanvar[:, n, :], stats[:, n, :])
                last.then_inc(ln_chain, 1)
                dve.wait_ge(ln_chain, c.at(2, 4))
                nc.vector.tensor_tensor(var_eps[:], meanvar[:, :, 1], eps[:], ALU.add).then_inc(var_ready, 1)

            def layernorm(c):
                dve.wait_ge(rstd_ready, c.at(1, 2))
                for n in range(NBLK):
                    last = nc.vector.tensor_scalar(xn[:, n, :], xin[:, n, :], meanvar[:, n, 0:1], rstd[:, n:n + 1],
                                                   ALU.subtract, ALU.mult)
                last.then_inc(xn_ready, 1)

            def job(c, s, back=0):
                kind, n = JOBS[s]
                bank = bank_of(s)
                src = jobp[bank]
                if kind in HI_KINDS:
                    dve.wait_ge(job_hi[bank], c.hi(s))
                else:
                    dve.wait_ge(job_ready[bank], c.job(s, back))
                if kind in ("q", "k"):
                    hi, lo, col = (q_hi, q_lo, n) if kind == "q" else (k_hi, k_lo, NPAIR + n)
                    done = nc.vector.scalar_tensor_tensor(
                        out=lo[:, n % 2, :], in0=src[:], scalar=bqk[:, col:col + 1],
                        in1=hi[:, n % 2, :].bitcast(F32), op0=ALU.add, op1=ALU.subtract)
                elif kind == "xt":
                    done = nc.vector.tensor_tensor(xt_lo[:], src[:], xt_hi[:].bitcast(F32), ALU.subtract)
                elif kind == "v":
                    cols = slice(S * (n // NBLK), S * (n // NBLK) + S)
                    done = nc.vector.scalar_tensor_tensor(
                        out=v_sb[:, n % NBLK, cols], in0=src[:], scalar=INV_SCALE, in1=bv8[:, cols],
                        op0=ALU.mult, op1=ALU.add)
                elif kind == "router":
                    rd = src[:, 0:NBLK * RPAD].rearrange("p (n r) -> p n r", r=RPAD)
                    nc.vector.tensor_tensor(u[:], rd[:, :, 0:PROJ],
                                            bp_b[:].unsqueeze(1).to_broadcast([P, NBLK, PROJ]), ALU.add)
                    done = nc.vector.tensor_copy(dn[:], rd[:, :, PROJ:NRD])
                else:
                    done = nc.vector.tensor_copy(gated_t[:], src[0:RSUM, :])
                done.then_inc(job_done[bank], 1)

            before = Counts(dve, -1)
            statistics(before)
            layernorm(before)

            links = [0]

            def link(ins):
                links[0] += 1
                ins.then_inc(setup_chain, 1)
                dve.wait_ge(setup_chain, links[0])

            for n, bank in enumerate(weight_banks):
                dve.wait_ge(w_hi_ready, n + 1)
                cols = slice(S * (n % 2), S * (n % 2) + S)
                nc.vector.tensor_tensor(w_lo[n // 2][:, cols], bank[:], w_hi[n // 2][:, cols].bitcast(F32),
                                        ALU.subtract).then_inc(w_lo_ready, 1)
            dve.wait_ge(small_bank_ready, 1)
            small = jobp[1]
            nc.vector.tensor_copy(wt[:], small[:, 0:P]).then_inc(small_ready, 1)
            nc.vector.tensor_copy(wrd[:], small[:, P:P + NRD]).then_inc(small_ready, 1)
            nc.vector.tensor_copy(wut[:], small[0:RSUM, 2 * P:3 * P]).then_inc(small_ready, 1)
            nc.vector.tensor_copy(bqk[:], small[:, 3 * P:3 * P + 2 * NPAIR]).then_inc(small_ready, 1)
            nc.vector.tensor_scalar(temp_c[:], temp_b[:], CLAMP_MAX, None, ALU.min).then_inc(temp_ready, 1)
            nc.vector.tensor_scalar(bv8[:], bv_b[:], INV_SCALE, None, ALU.mult)
            link(nc.vector.tensor_tensor(sim_sq[:], sim_b[:], sim_b[:], ALU.mult))
            nc.vector.tensor_reduce(sim_norm[:, 0, :], sim_sq[:].rearrange("p a b -> p b a"), AX_X, ALU.add)\
                .then_inc(simsq_ready, 1)
            dve.wait_ge(simnorm_ready, 1)
            link(nc.vector.tensor_scalar(sim_norm[:, 2, :], sim_norm[:, 1, :], L2_EPS, None, ALU.max))
            link(nc.vector.reciprocal(sim_norm[:, 3, :], sim_norm[:, 2, :]))
            link(nc.vector.tensor_tensor(sim_unit[:], sim_b[:].rearrange("p a b -> p b a"),
                                         sim_norm[:, 3, :].unsqueeze(2).to_broadcast([P, NEXP, PROJ]), ALU.mult))
            dve.wait_ge(gate_scale_ready, 1)
            link(nc.vector.tensor_scalar(simn[:], sim_unit[:], gate_scale[:, 0:1], None, ALU.mult))
            for s in AHEAD:
                job(before, s)

            def reciprocals(c, s):
                dve.wait_ge(p_ready, c.head(s, 1))
                nc.vector.reciprocal(rden[:, s % NROT, :], den[:, s % NROT, :]).then_inc(r_ready, 1)

            def maximum(c, s):
                cols = width(s)
                for h in range(2):
                    scored, read = c.fixed(c.head(s, h)), c.fixed(c.head(s - 2, h))
                    dve.wait_ge(consts_ready, 3)
                    dve.wait_ge(s_ready, scored)
                    wait(dve, p_ready, read)
                    nc.vector.tensor_tensor_reduce(
                        out=sm[:, s % 2, h, 0:cols], in0=scores[h][:, 0:cols], in1=mask[:, S - cols:S],
                        scale=-INV_SCALE, scalar=HUGE, op0=ALU.add, op1=ALU.min,
                        accum_out=nmax[:, s % NROT, h:h + 1]).then_inc(sm_ready, 1)

            def evacuate_pt(c, s):
                dve.wait_ge(t_ready, c.head(s, 1))
                i, p = s % NBLK, s // NBLK
                if i == 0:
                    wait(dve, pv_ready, c.pair(p - 2))
                src = ptp[1][:, 0:width(s)].rearrange("p (j q) -> p j q", q=P)
                nc.vector.tensor_copy(pt[:, p % 2, 1, 0:i + 1, P * i:P * i + P], src).then_inc(pt_ready[1], 1)

            def final(c):
                dve.wait_ge(o_ready, c.at(NQUAD, 0))
                dve.wait_ge(xres_loaded, c.at(16, 0))
                nc.vector.tensor_tensor(osb[:].rearrange("p n e -> p (n e)"), outp[:],
                                        xres[:].rearrange("p n e -> p (n e)"), ALU.add).then_inc(final_ready, 1)

            def router(c, s, chain):
                def link(ins):
                    chain[0] += 1
                    ins.then_inc(r_chain, 1)
                    dve.wait_ge(r_chain, c.at(R_CHAIN, chain[0]))

                def over_experts(t):
                    return t.unsqueeze(2).to_broadcast([P, NBLK, NEXP])

                if s == STEP_ROUTER + 2:
                    dve.wait_ge(job_done[bank_of(STEP_ROUTER)], c.job(STEP_ROUTER))
                    link(nc.vector.tensor_tensor(usq[:], u[:], u[:], ALU.mult))
                    nc.vector.tensor_reduce(unorm[:, 0, :], usq[:], AX_X, ALU.add).then_inc(unorm_ready, 1)
                    link(nc.vector.tensor_tensor(uprod[:], u[:].unsqueeze(2).to_broadcast([P, NBLK, NEXP, PROJ]),
                                                 simn[:].unsqueeze(1).to_broadcast([P, NBLK, NEXP, PROJ]), ALU.mult))
                    link(nc.vector.tensor_reduce(lg[:, 0, :, :], uprod[:], AX_X, ALU.add))
                if s == STEP_ROUTER + 4:
                    dve.wait_ge(unorm_root, c.at(1, 1))
                    link(nc.vector.tensor_scalar(unorm[:, 2, :], unorm[:, 1, :], L2_EPS, None, ALU.max))
                    link(nc.vector.reciprocal(unorm[:, 3, :], unorm[:, 2, :]))
                    link(nc.vector.tensor_tensor(lg[:, 1, :, :], lg[:, 0, :, :], over_experts(unorm[:, 3, :]), ALU.mult))
                    link(nc.vector.tensor_reduce(row[:, 0, :], lg[:, 1, :, :], AX_X, ALU.max))
                    nc.vector.tensor_tensor(lg[:, 2, :, :], lg[:, 1, :, :], over_experts(row[:, 0, :]), ALU.subtract)\
                        .then_inc(lg_ready, 1)
                if s == STEP_ROUTER + 7:
                    dve.wait_ge(lg_exp, c.at(1, 1))
                    link(nc.vector.tensor_reduce(row[:, 1, :], lg[:, 3, :, :], AX_X, ALU.add))
                    link(nc.vector.reciprocal(row[:, 2, :], row[:, 1, :]))
                    link(nc.vector.tensor_tensor(lg[:, 4, :, :], lg[:, 3, :, :], over_experts(row[:, 2, :]), ALU.mult))
                    link(nc.vector.tensor_reduce(row[:, 3, :], lg[:, 4, :, :], AX_X, ALU.max))
                    link(nc.vector.tensor_tensor(lg[:, 5, :, :], lg[:, 4, :, :], over_experts(row[:, 3, :]), ALU.is_ge))
                    taken = row[:, 4, :]
                    link(nc.vector.tensor_copy(taken, lg[:, 5, :, 0]))
                    for e in range(1, NEXP):
                        link(nc.vector.tensor_tensor(lg[:, 5, :, e], lg[:, 5, :, e], taken, ALU.is_gt))
                        link(nc.vector.tensor_tensor(taken, taken, lg[:, 5, :, e], ALU.max))
                    link(nc.vector.tensor_tensor(lg[:, 6, :, :], lg[:, 4, :, :], lg[:, 5, :, :], ALU.mult))
                    r0 = 0
                    for e, r in enumerate(RANKS):
                        last = nc.vector.tensor_tensor(gated[:, :, r0:r0 + r], dn[:, :, r0:r0 + r],
                                                       lg[:, 6, :, e:e + 1].to_broadcast([P, NBLK, r]), ALU.mult)
                        r0 += r
                    last.then_inc(gated_ready, 1)
                    assert chain[0] == R_CHAIN, chain

            def batch(b, first, last):
                c = Counts(dve, b)
                chain = [0]
                for s in range(UNITS):
                    if s > 0 or not first:
                        reciprocals(c, s - 1)
                    maximum(c, s)
                    if s >= LAG_T or not first:
                        evacuate_pt(c, s - LAG_T)
                    if s > 0 and s - 1 in JOBS and not (last and s - 1 in AHEAD):
                        job(c, s - 1)
                    if s == 0 and not first:
                        job(c, UNITS - 1, back=1)
                    if s == STEP_FINAL and not first:
                        final(c)
                    if s == STEP_STATS and not last:
                        statistics(c)
                    if s == STEP_NORM and not last:
                        layernorm(c)
                    router(c, s, chain)

            batch(0, True, False)
            with dve.Fori(1, NBATCH - 1) as b:
                batch(b, False, False)
            batch(NBATCH - 1, False, True)
            c = Counts(dve, NBATCH)
            reciprocals(c, -1)
            for s in range(LAG_T):
                evacuate_pt(c, s - LAG_T)
            final(c)

        @block.tensor
        def _(pe):
            def job(c, s):
                kind, n = JOBS[s]
                bank = bank_of(s)
                dst = jobp[bank]
                wait(pe, job_done[bank], c.job(s) - 1)
                if s in (28, 29, 30):
                    pe.wait_ge(job_done[0], c.job(26))
                if kind in ("q", "k"):
                    w = 0 if kind == "q" else 1
                    cols = slice(P * n, P * n + P)
                    for a, m in ((w_hi, xt_hi), (w_hi, xt_lo), (w_lo, xt_hi)):
                        tokens = m[:].rearrange("p (i q t) -> p i t q", q=P // 2, t=2) if kind == "q" else m[:]
                        done = nc.tensor.matmul(dst[:], a[w][:, cols], tokens, start=a is w_hi and m is xt_hi,
                                                stop=a is w_lo)
                elif kind == "v":
                    cols, keys = slice(S * (n // NBLK), S * (n // NBLK) + S), slice(P * (n % NBLK), P * (n % NBLK) + P)
                    for a, m in ((xt_hi, w_hi), (xt_hi, w_lo), (xt_lo, w_hi)):
                        done = nc.tensor.matmul(dst[:], a[:, keys], m[2][:, cols], start=a is xt_hi and m is w_hi,
                                                stop=a is xt_lo)
                elif kind == "xt":
                    pe.wait_ge(xn_ready, c.at(1, 2))
                    for i in range(NBLK):
                        done = nc.tensor.transpose(dst[:, P * i:P * i + P], xn[:, i, :], ident[:])
                elif kind == "router":
                    for i in range(NBLK):
                        done = nc.tensor.matmul(dst[:, RPAD * i:RPAD * i + NRD], xt[:, P * i:P * i + P], wrd[:],
                                                start=True, stop=True)
                else:
                    pe.wait_ge(gated_ready, c.at(1, 1))
                    for i in range(NBLK):
                        done = nc.tensor.transpose(dst[0:RSUM, P * i:P * i + P], gated[:, i, :], ident[:])
                done.then_inc(job_ready[bank], 1)

            pe.wait_ge(consts_ready, 1)
            for n, bank in enumerate(weight_banks):
                pe.wait_ge(w_loaded[n // 2], 16)
                for j in range(4):
                    last = nc.tensor.transpose(bank[:, P * j:P * j + P], w_in[n // 2][:, 4 * (n % 2) + j, :], ident[:])
                last.then_inc(wbank_ready, 1)
            pe.wait_ge(small_loaded, 16 * n_small)
            small = jobp[1]
            nc.tensor.transpose(small[:, 0:P], small_in[:, 0, :], ident[:])
            nc.tensor.transpose(small[:, P:P + NRD], small_in[0:NRD, 1, :], ident[0:NRD, 0:NRD])
            nc.tensor.transpose(small[0:RSUM, 2 * P:3 * P], small_in[:, 2, 0:RSUM], ident[:])
            nc.tensor.transpose(small[:, 3 * P:3 * P + 2 * NPAIR], small_in[0:2 * NPAIR, 3, :],
                                ident[0:2 * NPAIR, 0:2 * NPAIR]).then_inc(small_bank_ready, 1)
            pe.wait_ge(w_lo_ready, len(weight_banks))
            pe.wait_ge(small_ready, 4)
            for s in AHEAD:
                job(Counts(pe, -1), s)

            def score(c, s):
                i, p = s % NBLK, s // NBLK
                if i == 0:
                    for ahead in (4, 3):
                        js = (s - ahead) % UNITS
                        pe.wait_ge(job_done[bank_of(js)], c.job(js, back=int(s < ahead)))
                rows_i = slice(P * i, P * i + P)
                for n, (a, m) in enumerate(((q_hi, k_hi), (q_hi, k_lo), (q_lo, k_hi))):
                    for h in range(2):
                        if n == 0:
                            wait(pe, sm_ready, c.head(s - 1, h))
                        part = slice(DH * h, DH * h + DH)
                        done = nc.tensor.matmul(scores[h][:, 0:width(s)], a[part, p % 2, rows_i],
                                                m[part, p % 2, 0:width(s)], start=n == 0, stop=n == 2)
                        if n == 2:
                            done.then_inc(s_ready, 1)

            def transpose(c, s):
                for h in range(2):
                    pe.wait_ge(pn_ready, c.head(s, h))
                    wait(pe, pt_ready[h], c.unit(s - 1))
                    for j in range(s % NBLK + 1):
                        done = nc.tensor.transpose(ptp[h][:, P * j:P * j + P], prob[:, s % NROT, h, P * j:P * j + P],
                                                   ident[:])
                    done.then_inc(t_ready, 1)

            def values(c, p):
                for h in range(2):
                    pe.wait_ge(pt_ready[h], c.unit(NBLK * p + NBLK - 1))
                wait(pe, z_ready, c.pair(p - 1))
                if p == 0 or p == NPAIR // 2:
                    for js in V_STEPS[2:4] if p == 0 else V_STEPS[6:8]:
                        pe.wait_ge(job_done[bank_of(js)], c.job(js))
                for h in range(2):
                    col = DH * (2 * (p % NPAIR) + h)
                    z0 = S // 2 * h
                    for j in range(NBLK):
                        for odd in range(2):
                            seen = pt[:, p % 2, h, j, :].rearrange("p (i t q) -> p i t q", t=2, q=P // 2)[:, j:, odd, :]
                            done = nc.tensor.matmul(zp[DH * odd:DH * odd + DH, z0 + P // 2 * j:z0 + S // 2],
                                                    v_sb[:, j, col:col + DH], seen,
                                                    start=j == 0, stop=j == NBLK - 1)
                done.then_inc(pv_ready, 1)

            def project(c, g):
                pe.wait_ge(z_ready, c.pair(2 * g + 1))
                for n in range(NPAIR):
                    for h in range(QUAD):
                        done = nc.tensor.matmul(outp[ROWS * h:ROWS * h + ROWS, P * (g % NQUAD):P * (g % NQUAD) + P],
                                                zs[:, g % 2, h, n, :], projs[:, n, :],
                                                start=False, stop=False, skip_group_check=True)
                done.then_inc(o_ready, 1)

            def base(c):
                wait(pe, final_ready, c.at(1, 0))
                for i in range(NBLK):
                    cols = slice(P * i, P * i + P)
                    nc.tensor.matmul(outp[:, cols], xt[:, cols], wt[:], start=i == 0, stop=False,
                                     skip_group_check=True)

            def lora(c):
                pe.wait_ge(job_done[bank_of(STEP_GATED)], c.job(STEP_GATED))
                for i in range(NBLK):
                    cols = slice(P * i, P * i + P)
                    nc.tensor.matmul(outp[:, cols], gated_t[:, cols], wut[:], start=False, stop=False,
                                     skip_group_check=True)

            def batch(b, first, last):
                c = Counts(pe, b)
                for s in range(UNITS):
                    score(c, s)
                    if s >= LAG_T or not first:
                        transpose(c, s - LAG_T)
                    if s % NBLK == LAG_PV % NBLK and (s >= LAG_PV or not first):
                        values(c, (s - LAG_PV) // NBLK)
                    if s % (2 * NBLK) == LAG_OUT % (2 * NBLK) and (s >= LAG_OUT or not first):
                        project(c, (s - LAG_OUT) // (2 * NBLK))
                    if s == STEP_BASE:
                        base(c)
                    if s == STEP_LORA:
                        lora(c)
                    if s in JOBS and not (last and s in AHEAD):
                        job(c, s)

            batch(0, True, False)
            with pe.Fori(1, NBATCH - 1) as b:
                batch(b, False, False)
            batch(NBATCH - 1, False, True)
            c = Counts(pe, NBATCH)
            for s in range(STEP_FINAL):
                if s < LAG_T:
                    transpose(c, s - LAG_T)
                if s == LAG_PV % NBLK:
                    values(c, (s - LAG_PV) // NBLK)
                if s % (2 * NBLK) == LAG_OUT % (2 * NBLK):
                    project(c, (s - LAG_OUT) // (2 * NBLK))


_INS = ["x", "Wq", "bq", "Wk", "bk", "Wv", "bv", "proj"]
_FFN = ["W", "Wp", "bp", "sim", "temp"]
_NAMES = ([f"L0_attn_{n}" for n in _INS] + [f"L0_ffn_{n}" for n in _FFN]
          + [f"L0_ffn_Wd{n}" for n in range(NEXP)] + [f"L0_ffn_Wu{n}" for n in range(NEXP)])


def kernel(**inputs):
    import numpy as _np
    import concourse.bacc as _bacc
    from concourse import mybir as _mybir
    from concourse.bass_utils import run_bass_kernel_spmd as _run

    nc = _bacc.Bacc("TRN2", target_bir_lowering=False, num_devices=1)
    arrays, args = {}, []
    for name in _NAMES:
        a = _np.ascontiguousarray(inputs[name])
        arrays[f"in_{name}_dram"] = a
        args.append(nc.dram_tensor(f"in_{name}_dram", a.shape, _mybir.dt.from_np(a.dtype), kind="ExternalInput").ap())
    out = nc.dram_tensor("out_0_dram", (NBATCH, S, E), F32, kind="ExternalOutput").ap()
    build(nc, *args[:13], args[13:17], args[17:21], out)
    r = _run(nc, [arrays], core_ids=[0])
    return r.results[0]["out_0_dram"]
```

```python
from contextlib import ExitStack

import concourse.bass as bass
from concourse import mybir

F32 = mybir.dt.float32
F32R = mybir.dt.float32r
ALU = mybir.AluOpType
ACT = mybir.ActivationFunctionType
AX_X = mybir.AxisListType.X

P = 128
NBATCH, S, E = 16, 512, 128
H, DH = 16, 64
NPAIR = H // 2
NBLK = S // P
RANKS = (1, 2, 4, 8)
NEXP = len(RANKS)
RSUM = sum(RANKS)
PROJ = 32
NRD = PROJ + RSUM
RPAD = 48
LN_EPS = 1e-5
CLAMP_MAX = 4.605170185988092
L2_EPS = 1e-12
INV_SCALE = 1.0 / DH ** 0.5
MASKED = -1e30
HUGE = 3e38

UNITS = NPAIR * NBLK
QUAD = 4
NQUAD = H // QUAD
ROWS = S // H

LAG_T = 3
LAG_PV = (8, 10)
LAG_Z = (9, 11)
LAG_OUT = 15
NROT = 4

JOBS = {}
LEAD = {"k": NBLK, "q": NBLK + 1}
for _p in range(NPAIR):
    for _kind in LEAD:
        JOBS[(NBLK * _p - LEAD[_kind]) % UNITS] = (_kind, _p)
JOBS[6] = ("router", 0)
JOBS[25] = ("xt", 0)
JOBS[26] = ("gated", 0)
V_STEPS = (29, 30, 1, 5, 9, 13, 17, 21)
for _n, _s in enumerate(V_STEPS):
    JOBS[_s] = ("v", _n)
AHEAD = (25, 27, 28, 29, 30, 31)
KEY_STEPS = sorted(_s for _s in JOBS if JOBS[_s][0] == "k")
HI_KINDS = ("q", "k", "xt")

STEP_ROUTER, STEP_GATED = 6, 26
STEP_EVAC, STEP_BASE, STEP_OUT, STEP_FINAL, STEP_LORA = 12, 13, 14, 15, 29
STEPS_STATS, STEP_AGGR, STEP_VAR = (15, 19), 20, 21
STEP_PRODUCTS, STEP_UNORM, STEP_EXPERTS = 8, 13, 18
R_CHAIN = 18
R_FIRST = 23


def bank_of(s):
    return s % 2


def count_jobs(s, kinds=None):
    jobs = [j for j in JOBS if bank_of(j) == bank_of(s) and (kinds is None or JOBS[j][0] in kinds)]
    return len([j for j in jobs if j in AHEAD]) + len([j for j in jobs if j <= s]), len(jobs)


class Counts:

    def __init__(self, eng, b):
        self.eng, self.b, self.base = eng, b, {}

    def at(self, per_batch, k):
        if isinstance(self.b, int):
            return self.b * per_batch + k
        if per_batch not in self.base:
            self.base[per_batch] = self.eng.snap(self.b * per_batch)
        return self.base[per_batch] + k if k else self.base[per_batch]

    def fixed(self, value):
        if not isinstance(value, int):
            self.eng.compute_val(value)
        return value

    def head(self, s, h):
        return self.at(2 * UNITS, 2 * s + h + 1)

    def unit(self, s):
        return self.at(UNITS, s + 1)

    def values(self, p, h):
        return self.at(H, 2 * p + h + 1)

    def quad(self, g):
        return self.at(NQUAD, g + 1)

    def job(self, s, back=0):
        n, per_batch = count_jobs(s)
        return self.at(per_batch, n - back * per_batch)

    def hi(self, s, back=0):
        n, per_batch = count_jobs(s, HI_KINDS)
        return self.at(per_batch, n - back * per_batch)


def due(s, lag, every, first, tail):
    n, rest = divmod(s - lag, every)
    return None if rest or (first and n < 0) or (tail and n >= 0) else n


def wait(eng, semaphore, value):
    if not isinstance(value, int) or value > 0:
        eng.wait_ge(semaphore, value)


def own(h):
    return slice(DH * h, DH * h + DH)


def other(h):
    return own(1 - h)


def width(s):
    return P * (s % NBLK + 1)


def build(nc, x, Wq, bq, Wk, bk, Wv, bv, proj, W, Wp, bp, sim, temp, Wd, Wu, out):
    with ExitStack() as ctx:
        def sb(name, shape, dt=F32):
            return ctx.enter_context(nc.sbuf_tensor(name, shape, dt))

        def psum(name):
            return ctx.enter_context(nc.psum_tensor(name, [P, S], F32))

        def sem(name):
            return ctx.enter_context(nc.semaphore(name))

        scores = [psum(f"scores{h}") for h in range(2)]
        ptp = [psum(f"ptp{h}") for h in range(2)]
        zp = psum("zp")
        outp = psum("outp")
        jobp = [psum(f"jobp{n}") for n in range(2)]
        weight_banks = [*scores, *ptp, zp, outp]

        w_in = [sb(f"w_in{n}", [P, NPAIR, E]) for n in range(3)]
        w_hi = [sb(f"w_hi{n}", [P, H * DH], F32R) for n in range(3)]
        w_lo = [sb(f"w_lo{n}", [P, H * DH], F32R) for n in range(3)]
        projs = sb("projs", [P, NPAIR, E])
        small_in = sb("small_in", [P, 4, P])
        wt = sb("wt", [P, E])
        wrd = sb("wrd", [P, NRD])
        wut = sb("wut", [RSUM, E])
        bqk = sb("bqk", [P, 2 * NPAIR])
        bv_b = sb("bv_b", [P, H * DH])
        bv8 = sb("bv8", [P, H * DH])
        bp_b = sb("bp_b", [P, PROJ])
        sim_b = sb("sim_b", [P, PROJ, NEXP])
        sim_sq = sb("sim_sq", [P, PROJ, NEXP])
        sim_unit = sb("sim_unit", [P, NEXP, PROJ])
        simn = sb("simn", [P, NEXP, PROJ])
        sim_norm = sb("sim_norm", [P, 4, NEXP])
        temp_b = sb("temp_b", [P, 1])
        temp_c = sb("temp_c", [P, 1])
        gate_scale = sb("gate_scale", [P, 1])
        ident = sb("ident", [P, P])
        mask = sb("mask", [P, S])
        power = sb("power", [P, 2, NBLK])

        xin = sb("xin", [P, NBLK, E])
        stats = sb("stats", [P, NBLK, 6])
        meanvar = sb("meanvar", [P, NBLK, 2])
        eps = sb("eps", [P, NBLK])
        var_eps = sb("var_eps", [P, NBLK])
        rstd = sb("rstd", [P, NBLK])
        xc = sb("xc", [P, NBLK, E])
        xn = sb("xn", [P, NBLK, E])
        xt = sb("xt", [P, S])
        xt_hi = sb("xt_hi", [P, S], F32R)
        xt_lo = sb("xt_lo", [P, S], F32R)
        xres = sb("xres", [P, NBLK, E])
        osb = sb("osb", [P, NBLK, E])

        q_parts = sb("q_parts", [P, 2, 2, S], F32R)
        k_twice = sb("k_twice", [P, 2, 2, S], F32R)
        k_lo = sb("k_lo", [P, 2, S], F32R)
        v_sb = sb("v_sb", [P, NBLK, H * DH])
        sm = sb("sm", [P, 2, 2, S])
        nmax = sb("nmax", [P, NROT, 2])
        den = sb("den", [P, NROT, 2])
        rden = sb("rden", [P, NROT, 2])
        prob = sb("prob", [P, NROT, 2, S])
        pt = sb("pt", [P, 2, 2, NBLK, S])
        zs = sb("zs", [P, 2, NPAIR, QUAD, ROWS])
        y_t = sb("y_t", [P, S])

        u = sb("u", [P, NBLK, PROJ])
        dn = sb("dn", [P, NBLK, RSUM])
        usq = sb("usq", [P, NBLK, PROJ])
        unorm = sb("unorm", [P, 4, NBLK])
        uprod = sb("uprod", [P, NBLK, NEXP, PROJ])
        lg = sb("lg", [P, 7, NBLK, NEXP])
        row = sb("row", [P, 5, NBLK])
        gated = sb("gated", [P, NBLK, RSUM])
        gated_t = sb("gated_t", [RSUM, S])

        w_loaded = [sem(f"w_loaded{n}") for n in range(3)]
        small_loaded = sem("small_loaded")
        xin_loaded = sem("xin_loaded")
        xres_loaded = sem("xres_loaded")
        out_stored = sem("out_stored")
        zeroed = sem("zeroed")
        k_copied = sem("k_copied")
        consts_ready = sem("consts_ready")
        wbank_ready = sem("wbank_ready")
        w_hi_ready = sem("w_hi_ready")
        w_lo_ready = sem("w_lo_ready")
        small_bank_ready = sem("small_bank_ready")
        small_ready = sem("small_ready")
        setup_chain = sem("setup_chain")
        simsq_ready = sem("simsq_ready")
        simnorm_ready = sem("simnorm_ready")
        temp_ready = sem("temp_ready")
        gate_scale_ready = sem("gate_scale_ready")
        ln_chain = sem("ln_chain")
        var_ready = sem("var_ready")
        rstd_ready = sem("rstd_ready")
        xn_ready = sem("xn_ready")
        s_ready = sem("s_ready")
        sm_ready = sem("sm_ready")
        p_ready = sem("p_ready")
        r_ready = sem("r_ready")
        pn_ready = sem("pn_ready")
        t_ready = sem("t_ready")
        pt_ready = [sem(f"pt_ready{h}") for h in range(2)]
        pv_ready = sem("pv_ready")
        z_ready = sem("z_ready")
        o_ready = sem("o_ready")
        y_copied = sem("y_copied")
        y_ready = sem("y_ready")
        final_ready = sem("final_ready")
        job_ready = [sem(f"job_ready{n}") for n in range(2)]
        job_hi = [sem(f"job_hi{n}") for n in range(2)]
        job_done = [sem(f"job_done{n}") for n in range(2)]
        ln_centred = sem("ln_centred")
        products_ready = sem("products_ready")
        unorm_ready = sem("unorm_ready")
        unorm_root = sem("unorm_root")
        lg_ready = sem("lg_ready")
        lg_exp = sem("lg_exp")
        gated_ready = sem("gated_ready")
        r_chain = sem("r_chain")

        block = ctx.enter_context(nc.Block())
        n_small = 2 + 2 * NEXP + 7

        @block.sync
        def _(sp):
            def tok(t):
                return t.rearrange("(n p) e -> p n e", p=P)

            sp.dma_start(xin[:], tok(x[0])).then_inc(xin_loaded, 16)
            for n, w in enumerate((Wq, Wk, Wv)):
                sp.dma_start(w_in[n][:], w.rearrange("(c a) d e -> (a d) c e", a=2)).then_inc(w_loaded[n], 16)
            sp.dma_start(small_in[:, 0, :], W).then_inc(small_loaded, 16)
            sp.dma_start(small_in[0:PROJ, 1, :], Wp).then_inc(small_loaded, 16)
            r0 = 0
            for n, r in enumerate(RANKS):
                sp.dma_start(small_in[PROJ + r0:PROJ + r0 + r, 1, :], Wd[n]).then_inc(small_loaded, 16)
                sp.dma_start(small_in[:, 2, r0:r0 + r], Wu[n]).then_inc(small_loaded, 16)
                r0 += r
            for n, t in enumerate((bq, bk)):
                sp.dma_start(small_in[NPAIR * n:NPAIR * (n + 1), 3, :],
                             t.rearrange("(c a) d -> c (a d)", a=2)).then_inc(small_loaded, 16)
            sp.dma_start(bv_b[:], bv.rearrange("h d -> (h d)").partition_broadcast(P)).then_inc(small_loaded, 16)
            sp.dma_start(bp_b[:], bp.partition_broadcast(P)).then_inc(small_loaded, 16)
            sp.dma_start(sim_b[:].rearrange("p a b -> p (a b)"),
                         sim.rearrange("a b -> (a b)").partition_broadcast(P)).then_inc(small_loaded, 16)
            sp.dma_start(temp_b[:], temp.partition_broadcast(P)).then_inc(small_loaded, 16)
            sp.dma_start(projs[:], proj.rearrange("(c p) e -> p c e", p=P)).then_inc(small_loaded, 16)

            def rows(t, b):
                if isinstance(b, int):
                    return tok(t[b])
                return t[bass.ds(b, 1), :, :].rearrange("o (n p) e -> p (o n) e", p=P)

            def copy_keys(c, s):
                n = JOBS[s][1]
                sp.wait_ge(job_hi[bank_of(s)], c.hi(s))
                for h in range(2):
                    sp.dma_start(k_twice[other(h), h, n % 2, :].bitcast(F32),
                                 k_twice[own(h), h, n % 2, :].bitcast(F32)).then_inc(k_copied, 16)

            def batch(b):
                c = Counts(sp, b)
                first, last = b == 0 if isinstance(b, int) else False, b is last_batch
                if not last:
                    sp.wait_ge(xn_ready, c.at(1, 1))
                    sp.dma_start(xin[:], rows(x, b + 1)).then_inc(xin_loaded, 16)
                for s in KEY_STEPS:
                    if s < STEP_FINAL:
                        copy_keys(c, s)
                if not first:
                    sp.wait_ge(final_ready, c.at(1, 0))
                    sp.dma_start(rows(out, b - 1), osb[:]).then_inc(out_stored, 16)
                    sp.wait_ge(out_stored, c.at(16, 0))
                sp.dma_start(xres[:], rows(x, b)).then_inc(xres_loaded, 16)
                for s in KEY_STEPS:
                    if s >= STEP_FINAL and not (last and s in AHEAD):
                        copy_keys(c, s)

            last_batch = NBATCH - 1
            copy_keys(Counts(sp, -1), KEY_STEPS[-1])
            batch(0)
            with sp.Fori(1, last_batch) as b:
                batch(b)
            batch(last_batch)
            sp.wait_ge(final_ready, NBATCH)
            sp.dma_start(tok(out[last_batch]), osb[:]).then_inc(out_stored, 16)
            sp.wait_ge(out_stored, 16 * NBATCH)

        @block.gpsimd
        def _(pool):
            nc.gpsimd.memset(ident[:], 0.0).then_inc(zeroed, 1)
            nc.gpsimd.memset(mask[:], 0.0).then_inc(zeroed, 1)
            nc.gpsimd.memset(power[:, 0, :], -0.5).then_inc(zeroed, 1)
            nc.gpsimd.memset(power[:, 1, :], 0.5).then_inc(zeroed, 1)
            pool.wait_ge(zeroed, 4)
            nc.gpsimd.affine_select(out=ident[:], in_=ident[:], compare_op=ALU.not_equal, fill=1.0,
                                    base=0, pattern=[[-1, P]], channel_multiplier=1).then_inc(consts_ready, 1)
            for odd in range(2):
                pool.wait_ge(consts_ready, 1 + odd)
                diagonal = mask[64 * odd:64 * odd + 64, S - P:S]
                nc.gpsimd.affine_select(out=diagonal, in_=diagonal, compare_op=ALU.is_ge, fill=MASKED,
                                        base=odd, pattern=[[-1, P]], channel_multiplier=2).then_inc(consts_ready, 1)

            def layernorm(c):
                pool.wait_ge(var_ready, c.at(1, 2))
                nc.gpsimd.tensor_tensor(rstd[:], var_eps[:], power[:, 0, :], ALU.pow).then_inc(rstd_ready, 1)
                nc.gpsimd.tensor_tensor(xc[:], xin[:], meanvar[:, :, 0:1].to_broadcast([P, NBLK, E]), ALU.subtract)\
                    .then_inc(ln_centred, 1)
                pool.wait_ge(ln_centred, c.at(1, 2))
                pool.wait_ge(rstd_ready, c.at(1, 2))
                nc.gpsimd.tensor_tensor(xn[:], xc[:], rstd[:].unsqueeze(2).to_broadcast([P, NBLK, E]), ALU.mult)\
                    .then_inc(xn_ready, 1)

            pool.wait_ge(consts_ready, 3)
            layernorm(Counts(pool, -1))
            pool.wait_ge(simsq_ready, 1)
            nc.gpsimd.tensor_tensor(sim_norm[:, 1, :], sim_norm[:, 0, :], power[:, 1, 0:NEXP], ALU.pow)\
                .then_inc(simnorm_ready, 1)

            def normalise(c, s):
                pool.wait_ge(r_ready, c.unit(s))
                for h in range(2):
                    part = prob[:, s % NROT, h, 0:width(s)]
                    scale = rden[:, s % NROT, h:h + 1].to_broadcast([P, width(s)])
                    nc.gpsimd.tensor_tensor(part, part, scale, ALU.mult).then_inc(pn_ready, 1)

            def batch(b, last):
                c = Counts(pool, b)
                for s in range(UNITS):
                    if s == STEP_UNORM:
                        pool.wait_ge(unorm_ready, c.at(1, 1))
                        nc.gpsimd.tensor_tensor(unorm[:, 1, :], unorm[:, 0, :], power[:, 1, :], ALU.pow)\
                            .then_inc(unorm_root, 1)
                    if s == STEP_PRODUCTS:
                        pool.wait_ge(job_done[bank_of(STEP_ROUTER)], c.job(STEP_ROUTER))
                        nc.gpsimd.tensor_tensor(usq[:], u[:], u[:], ALU.mult)
                        nc.gpsimd.tensor_tensor(uprod[:], u[:].unsqueeze(2).to_broadcast([P, NBLK, NEXP, PROJ]),
                                                simn[:].unsqueeze(1).to_broadcast([P, NBLK, NEXP, PROJ]), ALU.mult)\
                            .then_inc(products_ready, 1)
                    normalise(c, s)
                    if s == STEP_VAR and not last:
                        layernorm(c)

            batch(0, False)
            with pool.Fori(1, NBATCH - 1) as b:
                batch(b, False)
            batch(NBATCH - 1, True)

        @block.scalar
        def _(act):
            for n, bank in enumerate(weight_banks):
                act.wait_ge(wbank_ready, n + 1)
                nc.scalar.activation(w_hi[n // 2][:, S * (n % 2):S * (n % 2) + S], bank[:], ACT.Copy)\
                    .then_inc(w_hi_ready, 1)
            act.wait_ge(temp_ready, 1)
            nc.scalar.activation(gate_scale[:], temp_c[:], ACT.Exp).then_inc(gate_scale_ready, 1)

            def job(c, s, back=0):
                kind, n = JOBS[s]
                bank = bank_of(s)
                if kind not in HI_KINDS:
                    return
                act.wait_ge(job_ready[bank], c.job(s, back))
                if kind == "xt":
                    nc.scalar.activation(xt_hi[:], jobp[bank][:], ACT.Copy)
                    nc.scalar.activation(xt[:], jobp[bank][:], ACT.Copy).then_inc(job_hi[bank], 1)
                else:
                    dst, col = (q_parts, n) if kind == "q" else (k_twice, NPAIR + n)
                    for h in range(2):
                        done = nc.scalar.activation(dst[own(h), h, n % 2, :], jobp[bank][own(h), :], ACT.Identity,
                                                    bias=bqk[own(h), col:col + 1])
                    done.then_inc(job_hi[bank], 1)

            def evacuate_z(c, p, h):
                act.wait_ge(pv_ready, c.values(p, h))
                if p % 2 == 0 and h == 0:
                    wait(act, o_ready, c.quad(p // 2 - 2))
                src = zp[:, S // 2 * h:S // 2 * (h + 1)].rearrange("p (r c) -> p c r", c=NPAIR)
                nc.scalar.activation(zs[:, p // 2 % 2, :, 2 * (p % 2) + h, :], src, ACT.Copy).then_inc(z_ready, 1)

            def evacuate_sum(c):
                act.wait_ge(o_ready, c.at(NQUAD, 0))
                nc.scalar.activation(y_t[:], outp[:], ACT.Copy).then_inc(y_copied, 1)

            def exponentials(c, s):
                for h in range(2):
                    act.wait_ge(sm_ready, c.head(s, h))
                    wait(act, t_ready, c.head(s - NROT, h))
                    nc.scalar.activation(prob[:, s % NROT, h, 0:width(s)], sm[:, s % 2, h, 0:width(s)], ACT.Exp,
                                         bias=nmax[:, s % NROT, h:h + 1], scale=-1.0,
                                         accum_out=den[:, s % NROT, h:h + 1]).then_inc(p_ready, 1)

            def evacuate_pt(c, s):
                act.wait_ge(t_ready, c.head(s, 0))
                i, p = s % NBLK, s // NBLK
                if i == 0:
                    wait(act, pv_ready, c.values(p - 2, 0))
                src = ptp[0][:, 0:width(s)].rearrange("p (j q) -> p j q", q=P)
                nc.scalar.activation(pt[:, p % 2, 0, 0:i + 1, P * i:P * i + P], src, ACT.Copy)\
                    .then_inc(pt_ready[0], 1)

            act.wait_ge(small_ready, 4)
            for s in AHEAD:
                job(Counts(act, -1), s)

            def step(c, s, first=False, last=False, tail=False):
                for h in range(2):
                    p = due(s, LAG_Z[h], NBLK, first, tail)
                    if p is not None:
                        evacuate_z(c, p, h)
                if not tail:
                    if s - 1 in JOBS and not (last and s - 1 in AHEAD):
                        job(c, s - 1)
                    if s == 0 and not first:
                        job(c, UNITS - 1, back=1)
                    if s == STEP_EXPERTS:
                        act.wait_ge(lg_ready, c.at(1, 1))
                        nc.scalar.activation(lg[:, 3, :, :], lg[:, 2, :, :], ACT.Exp).then_inc(lg_exp, 1)
                unit = due(s, LAG_T, 1, first, tail)
                if unit is not None:
                    evacuate_pt(c, unit)
                if not tail:
                    exponentials(c, s)
                if s == STEP_EVAC and not first:
                    evacuate_sum(c)

            def batch(b, first, last):
                c = Counts(act, b)
                for s in range(UNITS):
                    step(c, s, first, last)

            batch(0, True, False)
            with act.Fori(1, NBATCH - 1) as b:
                batch(b, False, False)
            batch(NBATCH - 1, False, True)
            c = Counts(act, NBATCH)
            for s in range(STEP_EVAC + 1):
                step(c, s, tail=True)

        @block.vector
        def _(dve):
            def statistics(c, half):
                dve.wait_ge(xin_loaded, c.at(16, 32))
                for n in range(2 * half, 2 * half + 2):
                    last = nc.vector.bn_stats(stats[:, n, :], xin[:, n, :])
                if half == 1:
                    last.then_inc(ln_chain, 1)

            def aggregates(c):
                dve.wait_ge(ln_chain, c.at(2, 3))
                nc.vector.memset(eps[:], LN_EPS)
                for n in range(NBLK):
                    last = nc.vector.bn_aggr(meanvar[:, n, :], stats[:, n, :])
                last.then_inc(ln_chain, 1)

            def variances(c):
                dve.wait_ge(ln_chain, c.at(2, 4))
                nc.vector.tensor_tensor(var_eps[:], meanvar[:, :, 1], eps[:], ALU.add).then_inc(var_ready, 1)

            def job(c, s, back=0):
                kind, n = JOBS[s]
                bank = bank_of(s)
                src = jobp[bank]
                if kind in HI_KINDS:
                    dve.wait_ge(job_hi[bank], c.hi(s, back))
                else:
                    dve.wait_ge(job_ready[bank], c.job(s, back))
                if kind in ("q", "k"):
                    hi, col = (q_parts, n) if kind == "q" else (k_twice, NPAIR + n)
                    for h in range(2):
                        lo = q_parts[other(h), h, n % 2, :] if kind == "q" else k_lo[own(h), n % 2, :]
                        done = nc.vector.scalar_tensor_tensor(
                            out=lo, in0=src[own(h), :], scalar=bqk[own(h), col:col + 1],
                            in1=hi[own(h), h, n % 2, :].bitcast(F32), op0=ALU.add, op1=ALU.subtract)
                elif kind == "xt":
                    done = nc.vector.tensor_tensor(xt_lo[:], src[:], xt_hi[:].bitcast(F32), ALU.subtract)
                elif kind == "v":
                    cols = slice(S * (n // NBLK), S * (n // NBLK) + S)
                    done = nc.vector.scalar_tensor_tensor(
                        out=v_sb[:, n % NBLK, cols], in0=src[:], scalar=INV_SCALE, in1=bv8[:, cols],
                        op0=ALU.mult, op1=ALU.add)
                elif kind == "router":
                    rd = src[:, 0:NBLK * RPAD].rearrange("p (n r) -> p n r", r=RPAD)
                    nc.vector.tensor_tensor(u[:], rd[:, :, 0:PROJ],
                                            bp_b[:].unsqueeze(1).to_broadcast([P, NBLK, PROJ]), ALU.add)
                    done = nc.vector.tensor_copy(dn[:], rd[:, :, PROJ:NRD])
                else:
                    done = nc.vector.tensor_copy(gated_t[:], src[0:RSUM, :])
                done.then_inc(job_done[bank], 1)

            before = Counts(dve, -1)
            for half in range(2):
                statistics(before, half)
            aggregates(before)
            variances(before)

            links = [0]

            def link(ins):
                links[0] += 1
                ins.then_inc(setup_chain, 1)
                dve.wait_ge(setup_chain, links[0])

            for n, bank in enumerate(weight_banks):
                dve.wait_ge(w_hi_ready, n + 1)
                cols = slice(S * (n % 2), S * (n % 2) + S)
                nc.vector.tensor_tensor(w_lo[n // 2][:, cols], bank[:], w_hi[n // 2][:, cols].bitcast(F32),
                                        ALU.subtract).then_inc(w_lo_ready, 1)
            dve.wait_ge(small_bank_ready, 1)
            small = jobp[1]
            nc.vector.tensor_copy(wt[:], small[:, 0:P]).then_inc(small_ready, 1)
            nc.vector.tensor_copy(wrd[:], small[:, P:P + NRD]).then_inc(small_ready, 1)
            nc.vector.tensor_copy(wut[:], small[0:RSUM, 2 * P:3 * P]).then_inc(small_ready, 1)
            nc.vector.tensor_copy(bqk[:], small[:, 3 * P:3 * P + 2 * NPAIR]).then_inc(small_ready, 1)
            nc.vector.tensor_scalar(temp_c[:], temp_b[:], CLAMP_MAX, None, ALU.min).then_inc(temp_ready, 1)
            nc.vector.tensor_scalar(bv8[:], bv_b[:], INV_SCALE, None, ALU.mult)
            link(nc.vector.tensor_tensor(sim_sq[:], sim_b[:], sim_b[:], ALU.mult))
            nc.vector.tensor_reduce(sim_norm[:, 0, :], sim_sq[:].rearrange("p a b -> p b a"), AX_X, ALU.add)\
                .then_inc(simsq_ready, 1)
            dve.wait_ge(simnorm_ready, 1)
            link(nc.vector.tensor_scalar(sim_norm[:, 2, :], sim_norm[:, 1, :], L2_EPS, None, ALU.max))
            link(nc.vector.reciprocal(sim_norm[:, 3, :], sim_norm[:, 2, :]))
            link(nc.vector.tensor_tensor(sim_unit[:], sim_b[:].rearrange("p a b -> p b a"),
                                         sim_norm[:, 3, :].unsqueeze(2).to_broadcast([P, NEXP, PROJ]), ALU.mult))
            dve.wait_ge(gate_scale_ready, 1)
            link(nc.vector.tensor_scalar(simn[:], sim_unit[:], gate_scale[:, 0:1], None, ALU.mult))
            for s in AHEAD:
                job(before, s)

            def reciprocals(c, s):
                dve.wait_ge(p_ready, c.head(s, 1))
                nc.vector.reciprocal(rden[:, s % NROT, :], den[:, s % NROT, :]).then_inc(r_ready, 1)

            def maximum(c, s):
                cols = width(s)
                for h in range(2):
                    scored, read = c.fixed(c.head(s, h)), c.fixed(c.head(s - 2, h))
                    dve.wait_ge(consts_ready, 3)
                    dve.wait_ge(s_ready, scored)
                    wait(dve, p_ready, read)
                    nc.vector.tensor_tensor_reduce(
                        out=sm[:, s % 2, h, 0:cols], in0=scores[h][:, 0:cols], in1=mask[:, S - cols:S],
                        scale=-INV_SCALE, scalar=HUGE, op0=ALU.add, op1=ALU.min,
                        accum_out=nmax[:, s % NROT, h:h + 1]).then_inc(sm_ready, 1)

            def evacuate_pt(c, s):
                dve.wait_ge(t_ready, c.head(s, 1))
                i, p = s % NBLK, s // NBLK
                if i == 0:
                    wait(dve, pv_ready, c.values(p - 2, 1))
                src = ptp[1][:, 0:width(s)].rearrange("p (j q) -> p j q", q=P)
                nc.vector.tensor_copy(pt[:, p % 2, 1, 0:i + 1, P * i:P * i + P], src).then_inc(pt_ready[1], 1)

            def final(c):
                dve.wait_ge(y_ready, c.at(1, 0))
                dve.wait_ge(xres_loaded, c.at(16, 0))
                nc.vector.tensor_tensor(osb[:].rearrange("p n e -> p (n e)"), jobp[bank_of(STEP_OUT)][:],
                                        xres[:].rearrange("p n e -> p (n e)"), ALU.add).then_inc(final_ready, 1)

            def router(c, t):
                def prior(n):
                    dve.wait_ge(r_chain, c.at(R_CHAIN, n))

                def over_experts(m):
                    return m.unsqueeze(2).to_broadcast([P, NBLK, NEXP])

                t -= R_FIRST
                logits, shifted, exps, weights, chosen, routed = (lg[:, n, :, :] for n in (1, 2, 3, 4, 5, 6))
                taken = row[:, 4, :]
                if t == 0:
                    dve.wait_ge(products_ready, c.at(1, 1))
                    nc.vector.tensor_reduce(unorm[:, 0, :], usq[:], AX_X, ALU.add).then_inc(unorm_ready, 1)
                    nc.vector.tensor_reduce(lg[:, 0, :, :], uprod[:], AX_X, ALU.add).then_inc(r_chain, 1)
                if t == 6:
                    dve.wait_ge(unorm_root, c.at(1, 1))
                    nc.vector.tensor_scalar(unorm[:, 2, :], unorm[:, 1, :], L2_EPS, None, ALU.max).then_inc(r_chain, 1)
                if t == 7:
                    prior(2)
                    nc.vector.reciprocal(unorm[:, 3, :], unorm[:, 2, :]).then_inc(r_chain, 1)
                if t == 8:
                    prior(3)
                    nc.vector.tensor_tensor(logits, lg[:, 0, :, :], over_experts(unorm[:, 3, :]), ALU.mult)\
                        .then_inc(r_chain, 1)
                if t == 9:
                    prior(4)
                    nc.vector.tensor_reduce(row[:, 0, :], logits, AX_X, ALU.max).then_inc(r_chain, 1)
                if t == 10:
                    prior(5)
                    nc.vector.tensor_tensor(shifted, logits, over_experts(row[:, 0, :]), ALU.subtract)\
                        .then_inc(lg_ready, 1)
                if t == 15:
                    dve.wait_ge(lg_exp, c.at(1, 1))
                    nc.vector.tensor_reduce(row[:, 1, :], exps, AX_X, ALU.add).then_inc(r_chain, 1)
                if t == 16:
                    prior(6)
                    nc.vector.reciprocal(row[:, 2, :], row[:, 1, :]).then_inc(r_chain, 1)
                if t == 17:
                    prior(7)
                    nc.vector.tensor_tensor(weights, exps, over_experts(row[:, 2, :]), ALU.mult).then_inc(r_chain, 1)
                if t == 18:
                    prior(8)
                    nc.vector.tensor_reduce(row[:, 3, :], weights, AX_X, ALU.max).then_inc(r_chain, 1)
                if t == 19:
                    prior(9)
                    nc.vector.tensor_tensor(chosen, weights, over_experts(row[:, 3, :]), ALU.is_ge)\
                        .then_inc(r_chain, 1)
                if t == 20:
                    prior(10)
                    nc.vector.tensor_copy(taken, lg[:, 5, :, 0]).then_inc(r_chain, 1)
                for e in range(1, NEXP):
                    if t == 19 + 2 * e:
                        prior(9 + 2 * e)
                        nc.vector.tensor_tensor(lg[:, 5, :, e], lg[:, 5, :, e], taken, ALU.is_gt).then_inc(r_chain, 1)
                    if t == 20 + 2 * e:
                        prior(10 + 2 * e)
                        nc.vector.tensor_tensor(taken, taken, lg[:, 5, :, e], ALU.max).then_inc(r_chain, 1)
                if t == 27:
                    prior(17)
                    nc.vector.tensor_tensor(routed, weights, chosen, ALU.mult).then_inc(r_chain, 1)
                if t == 28:
                    prior(18)
                    r0 = 0
                    for e, r in enumerate(RANKS):
                        last = nc.vector.tensor_tensor(gated[:, :, r0:r0 + r], dn[:, :, r0:r0 + r],
                                                       lg[:, 6, :, e:e + 1].to_broadcast([P, NBLK, r]), ALU.mult)
                        r0 += r
                    last.then_inc(gated_ready, 1)

            def step(c, s, first=False, last=False, tail=False):
                if not tail:
                    maximum(c, s)
                    router(c, 2 * s)
                unit = due(s, 1, 1, first, tail)
                if unit is not None:
                    reciprocals(c, unit)
                unit = due(s, LAG_T, 1, first, tail)
                if unit is not None:
                    evacuate_pt(c, unit)
                if s == STEP_FINAL and not first:
                    final(c)
                if tail:
                    return
                if s > 0 and s - 1 in JOBS and not (last and s - 1 in AHEAD):
                    job(c, s - 1)
                if s == 0 and not first:
                    job(c, UNITS - 1, back=1)
                if s in STEPS_STATS and not last:
                    statistics(c, STEPS_STATS.index(s))
                if s == STEP_AGGR and not last:
                    aggregates(c)
                if s == STEP_VAR and not last:
                    variances(c)
                router(c, 2 * s + 1)

            def batch(b, first, last):
                c = Counts(dve, b)
                for s in range(UNITS):
                    step(c, s, first, last)

            batch(0, True, False)
            with dve.Fori(1, NBATCH - 1) as b:
                batch(b, False, False)
            batch(NBATCH - 1, False, True)
            c = Counts(dve, NBATCH)
            for s in range(STEP_FINAL + 1):
                step(c, s, tail=True)

        @block.tensor
        def _(pe):
            def job(c, s):
                kind, n = JOBS[s]
                bank = bank_of(s)
                dst = jobp[bank]
                if s == STEP_OUT + 2:
                    wait(pe, final_ready, c.at(1, 0))
                wait(pe, job_done[bank], c.job(s) - 1)
                if kind in ("q", "k"):
                    w = 0 if kind == "q" else 1
                    cols = slice(P * n, P * n + P)
                    for a, m in ((w_hi, xt_hi), (w_hi, xt_lo), (w_lo, xt_hi)):
                        tokens = m[:].rearrange("p (i q t) -> p i t q", q=P // 2, t=2) if kind == "q" else m[:]
                        done = nc.tensor.matmul(dst[:], a[w][:, cols], tokens, start=a is w_hi and m is xt_hi,
                                                stop=a is w_lo)
                elif kind == "v":
                    cols, keys = slice(S * (n // NBLK), S * (n // NBLK) + S), slice(P * (n % NBLK), P * (n % NBLK) + P)
                    for a, m in ((xt_hi, w_hi), (xt_hi, w_lo), (xt_lo, w_hi)):
                        done = nc.tensor.matmul(dst[:], a[:, keys], m[2][:, cols], start=a is xt_hi and m is w_hi,
                                                stop=a is xt_lo)
                elif kind == "xt":
                    pe.wait_ge(xn_ready, c.at(1, 2))
                    for i in range(NBLK):
                        done = nc.tensor.transpose(dst[:, P * i:P * i + P], xn[:, i, :], ident[:])
                elif kind == "router":
                    for i in range(NBLK):
                        done = nc.tensor.matmul(dst[:, RPAD * i:RPAD * i + NRD], xt[:, P * i:P * i + P], wrd[:],
                                                start=True, stop=True)
                else:
                    pe.wait_ge(gated_ready, c.at(1, 1))
                    for i in range(NBLK):
                        done = nc.tensor.transpose(dst[0:RSUM, P * i:P * i + P], gated[:, i, :], ident[:])
                done.then_inc(job_ready[bank], 1)

            pe.wait_ge(consts_ready, 1)
            for n, bank in enumerate(weight_banks):
                pe.wait_ge(w_loaded[n // 2], 16)
                for j in range(4):
                    last = nc.tensor.transpose(bank[:, P * j:P * j + P], w_in[n // 2][:, 4 * (n % 2) + j, :], ident[:])
                last.then_inc(wbank_ready, 1)
            pe.wait_ge(small_loaded, 16 * n_small)
            small = jobp[1]
            nc.tensor.transpose(small[:, 0:P], small_in[:, 0, :], ident[:])
            nc.tensor.transpose(small[:, P:P + NRD], small_in[0:NRD, 1, :], ident[0:NRD, 0:NRD])
            nc.tensor.transpose(small[0:RSUM, 2 * P:3 * P], small_in[:, 2, 0:RSUM], ident[:])
            nc.tensor.transpose(small[:, 3 * P:3 * P + 2 * NPAIR], small_in[0:2 * NPAIR, 3, :],
                                ident[0:2 * NPAIR, 0:2 * NPAIR]).then_inc(small_bank_ready, 1)
            pe.wait_ge(w_lo_ready, len(weight_banks))
            pe.wait_ge(small_ready, 4)
            for s in AHEAD:
                job(Counts(pe, -1), s)

            def score(c, s):
                i, p = s % NBLK, s // NBLK
                if i == 0:
                    for ahead in LEAD.values():
                        js = (s - ahead) % UNITS
                        pe.wait_ge(job_done[bank_of(js)], c.job(js, back=int(s < ahead)))
                    pe.wait_ge(k_copied, c.at(32 * NPAIR, 32 * (p + 1)))
                queries = slice(P * i, P * i + P)
                for h in range(2):
                    wait(pe, sm_ready, c.head(s - 1, h))
                    nc.tensor.matmul(scores[h][:, 0:width(s)], q_parts[:, h, p % 2, queries],
                                     k_twice[:, h, p % 2, 0:width(s)], start=True, stop=False)
                for h in range(2):
                    nc.tensor.matmul(scores[h][:, 0:width(s)], q_parts[own(h), h, p % 2, queries],
                                     k_lo[own(h), p % 2, 0:width(s)], start=False, stop=True).then_inc(s_ready, 1)

            def transpose(c, s):
                for h in range(2):
                    pe.wait_ge(pn_ready, c.head(s, h))
                    wait(pe, pt_ready[h], c.unit(s - 1))
                    for j in range(s % NBLK + 1):
                        done = nc.tensor.transpose(ptp[h][:, P * j:P * j + P], prob[:, s % NROT, h, P * j:P * j + P],
                                                   ident[:])
                    done.then_inc(t_ready, 1)

            def values(c, p, h):
                pe.wait_ge(pt_ready[h], c.unit(NBLK * p + NBLK - 1))
                wait(pe, z_ready, c.values(p, h) - 1)
                if h == 0 and p in (0, NPAIR // 2):
                    for bank in range(2):
                        made = [js for js in V_STEPS[:4] if js not in AHEAD] if p == 0 else V_STEPS[4:]
                        made = [js for js in made if bank_of(js) == bank]
                        if made:
                            pe.wait_ge(job_done[bank], c.job(max(made)))
                col = DH * (2 * (p % NPAIR) + h)
                z0 = S // 2 * h
                for j in range(NBLK):
                    for odd in range(2):
                        seen = pt[:, p % 2, h, j, :].rearrange("p (i t q) -> p i t q", t=2, q=P // 2)[:, j:, odd, :]
                        done = nc.tensor.matmul(zp[DH * odd:DH * odd + DH, z0 + P // 2 * j:z0 + S // 2],
                                                v_sb[:, j, col:col + DH], seen, start=j == 0, stop=j == NBLK - 1)
                done.then_inc(pv_ready, 1)

            def project(c, g, half):
                pe.wait_ge(z_ready, c.values(2 * g + 1, 1))
                for n in range(NPAIR // 2 * half, NPAIR // 2 * (half + 1)):
                    done = nc.tensor.matmul(outp[:, P * (g % NQUAD):P * (g % NQUAD) + P], projs[:, n, :],
                                            zs[:, g % 2, n, :, :], start=False, stop=False, skip_group_check=True)
                if half == 1:
                    done.then_inc(o_ready, 1)

            def base(c):
                wait(pe, y_copied, c.at(1, 0))
                nc.tensor.matmul(outp[:], wt[:], xt[:], start=True, stop=False, skip_group_check=True)

            def lora(c):
                pe.wait_ge(job_done[bank_of(STEP_GATED)], c.job(STEP_GATED))
                nc.tensor.matmul(outp[:], wut[:], gated_t[:], start=False, stop=False, skip_group_check=True)

            def transpose_sum(c, tail):
                bank = bank_of(STEP_OUT)
                if not tail:
                    pe.wait_ge(job_done[bank], c.job(STEP_OUT))
                pe.wait_ge(y_copied, c.at(1, 0))
                for i in range(NBLK):
                    cols = slice(P * i, P * i + P)
                    done = nc.tensor.transpose(jobp[bank][:, cols], y_t[:, cols], ident[:])
                done.then_inc(y_ready, 1)

            def step(c, s, first=False, last=False, tail=False):
                if not tail:
                    score(c, s)
                unit = due(s, LAG_T, 1, first, tail)
                if unit is not None:
                    transpose(c, unit)
                for h in range(2):
                    p = due(s, LAG_PV[h], NBLK, first, tail)
                    if p is not None:
                        values(c, p, h)
                n = due(s, LAG_OUT, NBLK, first, tail)
                if n is not None:
                    project(c, n // 2, n % 2)
                if s == STEP_OUT and not first:
                    transpose_sum(c, tail)
                if tail:
                    return
                if s == STEP_BASE:
                    base(c)
                if s == STEP_LORA:
                    lora(c)
                if s in JOBS and not (last and s in AHEAD):
                    job(c, s)

            def batch(b, first, last):
                c = Counts(pe, b)
                for s in range(UNITS):
                    step(c, s, first, last)

            batch(0, True, False)
            with pe.Fori(1, NBATCH - 1) as b:
                batch(b, False, False)
            batch(NBATCH - 1, False, True)
            c = Counts(pe, NBATCH)
            for s in range(STEP_OUT + 1):
                step(c, s, tail=True)


_INS = ["x", "Wq", "bq", "Wk", "bk", "Wv", "bv", "proj"]
_FFN = ["W", "Wp", "bp", "sim", "temp"]
_NAMES = ([f"L0_attn_{n}" for n in _INS] + [f"L0_ffn_{n}" for n in _FFN]
          + [f"L0_ffn_Wd{n}" for n in range(NEXP)] + [f"L0_ffn_Wu{n}" for n in range(NEXP)])


def kernel(**inputs):
    import numpy as _np
    import concourse.bacc as _bacc
    from concourse import mybir as _mybir
    from concourse.bass_utils import run_bass_kernel_spmd as _run

    nc = _bacc.Bacc("TRN2", target_bir_lowering=False, num_devices=1)
    arrays, args = {}, []
    for name in _NAMES:
        a = _np.ascontiguousarray(inputs[name])
        arrays[f"in_{name}_dram"] = a
        args.append(nc.dram_tensor(f"in_{name}_dram", a.shape, _mybir.dt.from_np(a.dtype), kind="ExternalInput").ap())
    out = nc.dram_tensor("out_0_dram", (NBATCH, S, E), F32, kind="ExternalOutput").ap()
    build(nc, *args[:13], args[13:17], args[17:21], out)
    r = _run(nc, [arrays], core_ids=[0])
    return r.results[0]["out_0_dram"]
```

```python
from contextlib import ExitStack

import concourse.bass as bass
from concourse import mybir

F32 = mybir.dt.float32
F32R = mybir.dt.float32r
ALU = mybir.AluOpType
ACT = mybir.ActivationFunctionType
AX_X = mybir.AxisListType.X

P = 128
NBATCH, S, E = 16, 512, 128
H, DH = 16, 64
NPAIR = H // 2
NBLK = S // P
RANKS = (1, 2, 4, 8)
NEXP = len(RANKS)
RSUM = sum(RANKS)
PROJ = 32
NRD = PROJ + RSUM
RPAD = 48
PARTS, PART = 3, 32
LN_EPS = 1e-5
CLAMP_MAX = 4.605170185988092
L2_EPS = 1e-12
INV_SCALE = 1.0 / DH ** 0.5
MASKED = -1e30
HUGE = 3e38

UNITS = NPAIR * NBLK
OCT = 8
NOCT = H // OCT
OCT_PAIRS = OCT // 2
OCT_STEPS = OCT_PAIRS * NBLK
ROWS = S // H

LAG_T = 3
LAG_PV = (8, 10)
LAG_Z = (9, 11)
LAG_OUT = ((27, 31, 35, 39), (25, 27, 31, 35))
NROT = 4

JOBS = {}
LEAD = {"k": NBLK, "q": NBLK + 1}
for _p in range(NPAIR):
    for _kind in LEAD:
        JOBS[(NBLK * _p - LEAD[_kind]) % UNITS] = (_kind, _p)
JOBS[6] = ("router", 0)
JOBS[25] = ("xt", 0)
JOBS[26] = ("gated", 0)
V_STEPS = (29, 30, 1, 5, 9, 13, 17, 21)
for _n, _s in enumerate(V_STEPS):
    JOBS[_s] = ("v", _n)
AHEAD = (25, 27, 28, 29, 30, 31)
KEY_STEPS = sorted(_s for _s in JOBS if JOBS[_s][0] == "k")
HI_KINDS = ("q", "k", "xt")

STEP_ROUTER, STEP_GATED = 6, 26
STEP_EVAC, STEP_BASE, STEP_OUT, STEP_FINAL, STEP_LORA = 20, 23, 22, 23, 29
STEPS_STATS, STEP_AGGR, STEP_VAR = (15, 19), 20, 21
STEP_PRODUCTS, STEP_UNORM, STEP_EXPERTS = 8, 12, 17
R_CHAIN = 20
R_FIRST = 23


def bank_of(s):
    return s % 2


def count_jobs(s, kinds=None):
    jobs = [j for j in JOBS if bank_of(j) == bank_of(s) and (kinds is None or JOBS[j][0] in kinds)]
    return len([j for j in jobs if j in AHEAD]) + len([j for j in jobs if j <= s]), len(jobs)


class Counts:

    def __init__(self, eng, b):
        self.eng, self.b, self.base = eng, b, {}

    def at(self, per_batch, k):
        if isinstance(self.b, int):
            return self.b * per_batch + k
        if per_batch not in self.base:
            self.base[per_batch] = self.eng.snap(self.b * per_batch)
        return self.base[per_batch] + k if k else self.base[per_batch]

    def fixed(self, value):
        if not isinstance(value, int):
            self.eng.compute_val(value)
        return value

    def head(self, s, h):
        return self.at(2 * UNITS, 2 * s + h + 1)

    def unit(self, s):
        return self.at(UNITS, s + 1)

    def values(self, p, h):
        return self.at(H, 2 * p + h + 1)

    def oct(self, o):
        return self.at(NOCT, o + 1)

    def job(self, s, back=0):
        n, per_batch = count_jobs(s)
        return self.at(per_batch, n - back * per_batch)

    def hi(self, s, back=0):
        n, per_batch = count_jobs(s, HI_KINDS)
        return self.at(per_batch, n - back * per_batch)


def due(s, lag, every, first, tail):
    n, rest = divmod(s - lag, every)
    return None if rest or (first and n < 0) or (tail and n >= 0) else n


def wait(eng, semaphore, value):
    if not isinstance(value, int) or value > 0:
        eng.wait_ge(semaphore, value)


def own(h):
    return slice(DH * h, DH * h + DH)


def other(h):
    return own(1 - h)


def width(s):
    return P * (s % NBLK + 1)


def build(nc, x, Wq, bq, Wk, bk, Wv, bv, proj, W, Wp, bp, sim, temp, Wd, Wu, out):
    with ExitStack() as ctx:
        def sb(name, shape, dt=F32):
            return ctx.enter_context(nc.sbuf_tensor(name, shape, dt))

        def psum(name):
            return ctx.enter_context(nc.psum_tensor(name, [P, S], F32))

        def sem(name):
            return ctx.enter_context(nc.semaphore(name))

        scores = [psum(f"scores{h}") for h in range(2)]
        ptp = [psum(f"ptp{h}") for h in range(2)]
        zp = psum("zp")
        outp = psum("outp")
        jobp = [psum(f"jobp{n}") for n in range(2)]
        weight_banks = [*scores, *ptp, zp, outp]

        w_hi = [sb(f"w_hi{n}", [P, H * DH], F32R) for n in range(3)]
        w_lo = [sb(f"w_lo{n}", [P, H * DH], F32R) for n in range(3)]
        projs = sb("projs", [P, NPAIR, E])
        proj_hi = sb("proj_hi", [P, NPAIR, E], F32R)
        proj_lo = sb("proj_lo", [P, NPAIR, E], F32R)
        small_in = sb("small_in", [P, 3, P])
        bqk_in = sb("bqk_in", [2 * NPAIR, P])
        wt_hi = sb("wt_hi", [P, E], F32R)
        wt_lo = sb("wt_lo", [P, E], F32R)
        wrd = sb("wrd", [P, NRD])
        up_parts = sb("up_parts", [P, PARTS, PART], F32R)
        wut = sb("wut", [PARTS * PART, E], F32R)
        bqk = sb("bqk", [P, 2 * NPAIR])
        bv_b = sb("bv_b", [P, H * DH])
        bv8 = sb("bv8", [P, H * DH])
        bp_b = sb("bp_b", [P, PROJ])
        sim_b = sb("sim_b", [P, PROJ, NEXP])
        sim_sq = sb("sim_sq", [P, PROJ, NEXP])
        sim_unit = sb("sim_unit", [P, NEXP, PROJ])
        simn = sb("simn", [P, NEXP, PROJ])
        sim_norm = sb("sim_norm", [P, 4, NEXP])
        temp_b = sb("temp_b", [P, 1])
        temp_c = sb("temp_c", [P, 1])
        gate_scale = sb("gate_scale", [P, 1])
        ident = sb("ident", [P, P])
        mask = sb("mask", [P, S])
        power = sb("power", [P, 2, NBLK])

        xin = sb("xin", [P, NBLK, E])
        stats = sb("stats", [P, NBLK, 6])
        meanvar = sb("meanvar", [P, NBLK, 2])
        eps = sb("eps", [P, NBLK])
        var_eps = sb("var_eps", [P, NBLK])
        rstd = sb("rstd", [P, NBLK])
        xc = sb("xc", [P, NBLK, E])
        xn = sb("xn", [P, NBLK, E])
        xt = sb("xt", [P, S])
        xt_hi = sb("xt_hi", [P, S], F32R)
        xt_lo = sb("xt_lo", [P, S], F32R)
        xres = sb("xres", [P, NBLK, E])
        osb = sb("osb", [P, NBLK, E])

        q_parts = sb("q_parts", [P, 2, 2, S], F32R)
        k_twice = sb("k_twice", [P, 2, 2, S], F32R)
        k_hi = sb("k_hi", [P, 2, S], F32R)
        k_lo = sb("k_lo", [P, 2, S], F32R)
        v_sb = sb("v_sb", [P, NBLK, H * DH])
        sm = sb("sm", [P, 2, 2, S])
        nmax = sb("nmax", [P, NROT, 2])
        den = sb("den", [P, NROT, 2])
        rden = sb("rden", [P, NROT, 2])
        prob = sb("prob", [P, NROT, 2, S])
        pt = sb("pt", [P, 2, 2, NBLK, S])
        w_in = [pt[:, n // 2, n % 2, 0:2, :].rearrange("p a (c e) -> p (a c) e", e=E) for n in range(3)]
        z_hi = sb("z_hi", [P, 2, NPAIR, OCT, ROWS], F32R)
        z_lo = sb("z_lo", [P, 2, NPAIR, OCT, ROWS], F32R)
        y_t = sb("y_t", [P, S])

        u = sb("u", [P, NBLK, PROJ])
        dn = sb("dn", [P, NBLK, RSUM])
        usq = sb("usq", [P, NBLK, PROJ])
        unorm = sb("unorm", [P, 4, NBLK])
        uprod = sb("uprod", [P, NBLK, NEXP, PROJ])
        lg = sb("lg", [P, 7, NBLK, NEXP])
        row = sb("row", [P, 5, NBLK])
        gated = sb("gated", [P, NBLK, RSUM])
        gated_parts = sb("gated_parts", [P, NBLK, PARTS, PART], F32R)
        gated_t = sb("gated_t", [PARTS * PART, S], F32R)

        w_loaded = [sem(f"w_loaded{n}") for n in range(3)]
        bqk_loaded = sem("bqk_loaded")
        proj_loaded = sem("proj_loaded")
        proj_split = sem("proj_split")
        bv_loaded = sem("bv_loaded")
        sim_loaded = sem("sim_loaded")
        small_loaded = sem("small_loaded")
        xin_loaded = sem("xin_loaded")
        xres_loaded = sem("xres_loaded")
        out_stored = sem("out_stored")
        zeroed = sem("zeroed")
        k_copied = sem("k_copied")
        consts_ready = sem("consts_ready")
        wbank_ready = sem("wbank_ready")
        w_hi_ready = sem("w_hi_ready")
        w_lo_ready = sem("w_lo_ready")
        up_ready = sem("up_ready")
        bqk_bank_ready = sem("bqk_bank_ready")
        bqk_ready = sem("bqk_ready")
        small_bank_ready = sem("small_bank_ready")
        small_ready = sem("small_ready")
        setup_chain = sem("setup_chain")
        simsq_ready = sem("simsq_ready")
        simnorm_ready = sem("simnorm_ready")
        simn_ready = sem("simn_ready")
        temp_ready = sem("temp_ready")
        gate_scale_ready = sem("gate_scale_ready")
        ln_chain = sem("ln_chain")
        var_ready = sem("var_ready")
        rstd_ready = sem("rstd_ready")
        xn_ready = sem("xn_ready")
        s_ready = sem("s_ready")
        sm_ready = sem("sm_ready")
        p_ready = sem("p_ready")
        r_ready = sem("r_ready")
        pn_ready = sem("pn_ready")
        t_ready = sem("t_ready")
        pt_ready = [sem(f"pt_ready{h}") for h in range(2)]
        pv_ready = sem("pv_ready")
        z_hi_ready = sem("z_hi_ready")
        z_ready = sem("z_ready")
        o_ready = sem("o_ready")
        y_copied = sem("y_copied")
        y_ready = sem("y_ready")
        final_ready = sem("final_ready")
        job_ready = [sem(f"job_ready{n}") for n in range(2)]
        job_hi = [sem(f"job_hi{n}") for n in range(2)]
        job_done = [sem(f"job_done{n}") for n in range(2)]
        ln_centred = sem("ln_centred")
        products_ready = sem("products_ready")
        unorm_ready = sem("unorm_ready")
        unorm_root = sem("unorm_root")
        lg_ready = sem("lg_ready")
        lg_exp = sem("lg_exp")
        gated_ready = sem("gated_ready")
        r_chain = sem("r_chain")

        def z_views(p, h):
            half = zp[:, S // 2 * h:S // 2 * (h + 1)].rearrange("p (r c) -> p c r", c=NPAIR)
            o, head = p // OCT_PAIRS % 2, 2 * (p % OCT_PAIRS) + h
            return z_hi[:, o, :, head, :], half, z_lo[:, o, :, head, :]

        block = ctx.enter_context(nc.Block())
        n_small = 3 + 2 * NEXP

        @block.sync
        def _(sp):
            def tok(t):
                return t.rearrange("(n p) e -> p n e", p=P)

            sp.dma_start(xin[:], tok(x[0])).then_inc(xin_loaded, 16)

            def load_weights(n, w):
                sp.dma_start(w_in[n], w.rearrange("(c a) d e -> (a d) c e", a=2)).then_inc(w_loaded[n], 16)

            load_weights(0, Wq)
            for n, t in enumerate((bq, bk)):
                sp.dma_start(bqk_in[NPAIR * n:NPAIR * (n + 1), :],
                             t.rearrange("(c a) d -> c (a d)", a=2)).then_inc(bqk_loaded, 16)
            load_weights(1, Wk)
            sp.dma_start(sim_b[:].rearrange("p a b -> p (a b)"),
                         sim.rearrange("a b -> (a b)").partition_broadcast(P)).then_inc(sim_loaded, 16)
            sp.dma_start(temp_b[:], temp.partition_broadcast(P)).then_inc(sim_loaded, 16)
            load_weights(2, Wv)
            sp.dma_start(bv_b[:], bv.rearrange("h d -> (h d)").partition_broadcast(P)).then_inc(bv_loaded, 16)
            sp.dma_start(small_in[:, 0, :], W).then_inc(small_loaded, 16)
            sp.dma_start(small_in[0:PROJ, 1, :], Wp).then_inc(small_loaded, 16)
            r0 = 0
            for n, r in enumerate(RANKS):
                sp.dma_start(small_in[PROJ + r0:PROJ + r0 + r, 1, :], Wd[n]).then_inc(small_loaded, 16)
                sp.dma_start(small_in[:, 2, r0:r0 + r], Wu[n]).then_inc(small_loaded, 16)
                r0 += r
            sp.dma_start(bp_b[:], bp.partition_broadcast(P)).then_inc(small_loaded, 16)
            sp.dma_start(projs[:], proj.rearrange("(c p) e -> p c e", p=P)).then_inc(proj_loaded, 16)

            def rows(t, b):
                if isinstance(b, int):
                    return tok(t[b])
                return t[bass.ds(b, 1), :, :].rearrange("o (n p) e -> p (o n) e", p=P)

            def copy_keys(c, s):
                n = JOBS[s][1]
                sp.wait_ge(job_hi[bank_of(s)], c.hi(s))
                for h in range(2):
                    for half in (own(h), other(h)):
                        sp.dma_start(k_twice[half, h, n % 2, :].bitcast(F32),
                                     k_hi[own(h), n % 2, :].bitcast(F32)).then_inc(k_copied, 16)

            def batch(b):
                c = Counts(sp, b)
                first, last = b == 0 if isinstance(b, int) else False, b is last_batch
                if not last:
                    sp.wait_ge(xn_ready, c.at(1, 1))
                    sp.dma_start(xin[:], rows(x, b + 1)).then_inc(xin_loaded, 16)
                for s in KEY_STEPS:
                    if s < STEP_FINAL:
                        copy_keys(c, s)
                if not first:
                    sp.wait_ge(final_ready, c.at(1, 0))
                    sp.dma_start(rows(out, b - 1), osb[:]).then_inc(out_stored, 16)
                    sp.wait_ge(out_stored, c.at(16, 0))
                sp.dma_start(xres[:], rows(x, b)).then_inc(xres_loaded, 16)
                for s in KEY_STEPS:
                    if s >= STEP_FINAL and not (last and s in AHEAD):
                        copy_keys(c, s)

            last_batch = NBATCH - 1
            copy_keys(Counts(sp, -1), KEY_STEPS[-1])
            batch(0)
            with sp.Fori(1, last_batch) as b:
                batch(b)
            batch(last_batch)
            sp.wait_ge(final_ready, NBATCH)
            sp.dma_start(tok(out[last_batch]), osb[:]).then_inc(out_stored, 16)
            sp.wait_ge(out_stored, 16 * NBATCH)

        @block.gpsimd
        def _(pool):
            nc.gpsimd.memset(ident[:], 0.0).then_inc(zeroed, 1)
            nc.gpsimd.memset(mask[:], 0.0).then_inc(zeroed, 1)
            nc.gpsimd.memset(power[:, 0, :], -0.5).then_inc(zeroed, 1)
            nc.gpsimd.memset(power[:, 1, :], 0.5).then_inc(zeroed, 1)
            nc.gpsimd.memset(gated_parts[:].bitcast(F32), 0.0).then_inc(zeroed, 1)
            nc.gpsimd.memset(up_parts[:].bitcast(F32), 0.0).then_inc(zeroed, 1)
            pool.wait_ge(zeroed, 6)
            nc.gpsimd.affine_select(out=ident[:], in_=ident[:], compare_op=ALU.not_equal, fill=1.0,
                                    base=0, pattern=[[-1, P]], channel_multiplier=1).then_inc(consts_ready, 1)
            for odd in range(2):
                pool.wait_ge(consts_ready, 1 + odd)
                diagonal = mask[64 * odd:64 * odd + 64, S - P:S]
                nc.gpsimd.affine_select(out=diagonal, in_=diagonal, compare_op=ALU.is_ge, fill=MASKED,
                                        base=odd, pattern=[[-1, P]], channel_multiplier=2).then_inc(consts_ready, 1)

            def layernorm(c):
                pool.wait_ge(var_ready, c.at(1, 2))
                nc.gpsimd.tensor_tensor(rstd[:], var_eps[:], power[:, 0, :], ALU.pow).then_inc(rstd_ready, 1)
                nc.gpsimd.tensor_tensor(xc[:], xin[:], meanvar[:, :, 0:1].to_broadcast([P, NBLK, E]), ALU.subtract)\
                    .then_inc(ln_centred, 1)
                pool.wait_ge(ln_centred, c.at(1, 2))
                pool.wait_ge(rstd_ready, c.at(1, 2))
                nc.gpsimd.tensor_tensor(xn[:], xc[:], rstd[:].unsqueeze(2).to_broadcast([P, NBLK, E]), ALU.mult)\
                    .then_inc(xn_ready, 1)

            pool.wait_ge(consts_ready, 3)
            layernorm(Counts(pool, -1))
            pool.wait_ge(proj_loaded, 16)
            nc.gpsimd.tensor_copy(proj_hi[:], projs[:]).then_inc(proj_split, 1)
            pool.wait_ge(proj_split, 1)
            nc.gpsimd.tensor_tensor(proj_lo[:], projs[:], proj_hi[:].bitcast(F32), ALU.subtract).then_inc(proj_split, 1)
            pool.wait_ge(simsq_ready, 1)
            nc.gpsimd.tensor_tensor(sim_norm[:, 1, :], sim_norm[:, 0, :], power[:, 1, 0:NEXP], ALU.pow)\
                .then_inc(simnorm_ready, 1)

            def normalise(c, s):
                pool.wait_ge(r_ready, c.unit(s))
                for h in range(2):
                    part = prob[:, s % NROT, h, 0:width(s)]
                    scale = rden[:, s % NROT, h:h + 1].to_broadcast([P, width(s)])
                    nc.gpsimd.tensor_tensor(part, part, scale, ALU.mult).then_inc(pn_ready, 1)

            def batch(b, last):
                c = Counts(pool, b)
                for s in range(UNITS):
                    if s == STEP_UNORM:
                        pool.wait_ge(unorm_ready, c.at(1, 1))
                        nc.gpsimd.tensor_tensor(unorm[:, 1, :], unorm[:, 0, :], power[:, 1, :], ALU.pow)\
                            .then_inc(unorm_root, 1)
                    if s == STEP_PRODUCTS:
                        pool.wait_ge(simn_ready, 1)
                        pool.wait_ge(job_done[bank_of(STEP_ROUTER)], c.job(STEP_ROUTER))
                        nc.gpsimd.tensor_tensor(usq[:], u[:], u[:], ALU.mult)
                        nc.gpsimd.tensor_tensor(uprod[:], u[:].unsqueeze(2).to_broadcast([P, NBLK, NEXP, PROJ]),
                                                simn[:].unsqueeze(1).to_broadcast([P, NBLK, NEXP, PROJ]), ALU.mult)\
                            .then_inc(products_ready, 1)
                    normalise(c, s)
                    if s == STEP_VAR and not last:
                        layernorm(c)

            batch(0, False)
            with pool.Fori(1, NBATCH - 1) as b:
                batch(b, False)
            batch(NBATCH - 1, True)

        @block.scalar
        def _(act):
            def weights(n):
                for bank in (2 * n, 2 * n + 1):
                    act.wait_ge(wbank_ready, bank + 1)
                    nc.scalar.activation(w_hi[n][:, S * (bank % 2):S * (bank % 2) + S], weight_banks[bank][:], ACT.Copy)\
                        .then_inc(w_hi_ready, 1)

            def job(c, s, back=0):
                kind, n = JOBS[s]
                bank = bank_of(s)
                if kind not in HI_KINDS:
                    return
                act.wait_ge(job_ready[bank], c.job(s, back))
                if kind == "xt":
                    nc.scalar.activation(xt_hi[:], jobp[bank][:], ACT.Copy)
                    nc.scalar.activation(xt[:], jobp[bank][:], ACT.Copy).then_inc(job_hi[bank], 1)
                elif kind == "k":
                    nc.scalar.activation(k_hi[:, n % 2, :], jobp[bank][:], ACT.Identity,
                                         bias=bqk[:, NPAIR + n:NPAIR + n + 1]).then_inc(job_hi[bank], 1)
                else:
                    for h in range(2):
                        done = nc.scalar.activation(q_parts[own(h), h, n % 2, :], jobp[bank][own(h), :],
                                                    ACT.Identity, bias=bqk[own(h), n:n + 1])
                    done.then_inc(job_hi[bank], 1)

            def evacuate_z(c, p, h):
                act.wait_ge(pv_ready, c.values(p, h))
                if p % OCT_PAIRS == 0 and h == 0:
                    wait(act, o_ready, c.oct(p // OCT_PAIRS - 2))
                high, half, _ = z_views(p, h)
                nc.scalar.activation(high, half, ACT.Copy).then_inc(z_hi_ready, 1)

            def evacuate_sum(c):
                act.wait_ge(o_ready, c.at(NOCT, 0))
                nc.scalar.activation(y_t[:], outp[:], ACT.Copy).then_inc(y_copied, 1)

            def exponentials(c, s):
                for h in range(2):
                    act.wait_ge(sm_ready, c.head(s, h))
                    wait(act, t_ready, c.head(s - NROT, h))
                    nc.scalar.activation(prob[:, s % NROT, h, 0:width(s)], sm[:, s % 2, h, 0:width(s)], ACT.Exp,
                                         bias=nmax[:, s % NROT, h:h + 1], scale=-1.0,
                                         accum_out=den[:, s % NROT, h:h + 1]).then_inc(p_ready, 1)

            def evacuate_pt(c, s):
                act.wait_ge(t_ready, c.head(s, 0))
                i, p = s % NBLK, s // NBLK
                if i == 0:
                    wait(act, pv_ready, c.values(p - 2, 0))
                src = ptp[0][:, 0:width(s)].rearrange("p (j q) -> p j q", q=P)
                nc.scalar.activation(pt[:, p % 2, 0, 0:i + 1, P * i:P * i + P], src, ACT.Copy)\
                    .then_inc(pt_ready[0], 1)

            weights(0)
            weights(1)
            act.wait_ge(bqk_ready, 1)
            for s in AHEAD:
                job(Counts(act, -1), s)
                if JOBS[s][0] == "xt":
                    weights(2)
                if JOBS[s][0] == "k":
                    act.wait_ge(temp_ready, 1)
                    nc.scalar.activation(gate_scale[:], temp_c[:], ACT.Exp).then_inc(gate_scale_ready, 1)

            def step(c, s, first=False, last=False, tail=False):
                for h in range(2):
                    p = due(s, LAG_Z[h], NBLK, first, tail)
                    if p is not None:
                        evacuate_z(c, p, h)
                if not tail:
                    if s - 1 in JOBS and not (last and s - 1 in AHEAD):
                        job(c, s - 1)
                    if s == 0 and not first:
                        job(c, UNITS - 1, back=1)
                    if s == STEP_EXPERTS:
                        act.wait_ge(lg_ready, c.at(1, 1))
                        nc.scalar.activation(lg[:, 3, :, :], lg[:, 2, :, :], ACT.Exp).then_inc(lg_exp, 1)
                unit = due(s, LAG_T, 1, first, tail)
                if unit is not None:
                    evacuate_pt(c, unit)
                if not tail:
                    exponentials(c, s)
                if s == STEP_EVAC and not first:
                    evacuate_sum(c)

            def batch(b, first, last):
                c = Counts(act, b)
                for s in range(UNITS):
                    step(c, s, first, last)

            batch(0, True, False)
            with act.Fori(1, NBATCH - 1) as b:
                batch(b, False, False)
            batch(NBATCH - 1, False, True)
            c = Counts(act, NBATCH)
            for s in range(STEP_EVAC + 1):
                step(c, s, tail=True)

        @block.vector
        def _(dve):
            def statistics(c, half):
                dve.wait_ge(xin_loaded, c.at(16, 32))
                for n in range(2 * half, 2 * half + 2):
                    last = nc.vector.bn_stats(stats[:, n, :], xin[:, n, :])
                if half == 1:
                    last.then_inc(ln_chain, 1)

            def aggregates(c):
                dve.wait_ge(ln_chain, c.at(2, 3))
                nc.vector.memset(eps[:], LN_EPS)
                for n in range(NBLK):
                    last = nc.vector.bn_aggr(meanvar[:, n, :], stats[:, n, :])
                last.then_inc(ln_chain, 1)

            def variances(c):
                dve.wait_ge(ln_chain, c.at(2, 4))
                nc.vector.tensor_tensor(var_eps[:], meanvar[:, :, 1], eps[:], ALU.add).then_inc(var_ready, 1)

            def job(c, s, back=0):
                kind, n = JOBS[s]
                bank = bank_of(s)
                src = jobp[bank]
                if kind in HI_KINDS:
                    dve.wait_ge(job_hi[bank], c.hi(s, back))
                else:
                    dve.wait_ge(job_ready[bank], c.job(s, back))
                if kind == "k":
                    done = nc.vector.scalar_tensor_tensor(
                        out=k_lo[:, n % 2, :], in0=src[:], scalar=bqk[:, NPAIR + n:NPAIR + n + 1],
                        in1=k_hi[:, n % 2, :].bitcast(F32), op0=ALU.add, op1=ALU.subtract)
                elif kind == "q":
                    for h in range(2):
                        done = nc.vector.scalar_tensor_tensor(
                            out=q_parts[other(h), h, n % 2, :], in0=src[own(h), :], scalar=bqk[own(h), n:n + 1],
                            in1=q_parts[own(h), h, n % 2, :].bitcast(F32), op0=ALU.add, op1=ALU.subtract)
                elif kind == "xt":
                    done = nc.vector.tensor_tensor(xt_lo[:], src[:], xt_hi[:].bitcast(F32), ALU.subtract)
                elif kind == "v":
                    cols = slice(S * (n // NBLK), S * (n // NBLK) + S)
                    done = nc.vector.scalar_tensor_tensor(
                        out=v_sb[:, n % NBLK, cols], in0=src[:], scalar=INV_SCALE, in1=bv8[:, cols],
                        op0=ALU.mult, op1=ALU.add)
                elif kind == "router":
                    rd = src[:, 0:NBLK * RPAD].rearrange("p (n r) -> p n r", r=RPAD)
                    nc.vector.tensor_tensor(u[:], rd[:, :, 0:PROJ],
                                            bp_b[:].unsqueeze(1).to_broadcast([P, NBLK, PROJ]), ALU.add)
                    done = nc.vector.tensor_copy(dn[:], rd[:, :, PROJ:NRD])
                else:
                    done = nc.vector.tensor_copy(gated_t[:], src[0:PARTS * PART, :])
                done.then_inc(job_done[bank], 1)

            before = Counts(dve, -1)
            for half in range(2):
                statistics(before, half)
            aggregates(before)
            variances(before)

            links = [0]

            def link(ins):
                links[0] += 1
                ins.then_inc(setup_chain, 1)
                dve.wait_ge(setup_chain, links[0])

            def weights(n):
                for bank in (2 * n, 2 * n + 1):
                    dve.wait_ge(w_hi_ready, bank + 1)
                    cols = slice(S * (bank % 2), S * (bank % 2) + S)
                    nc.vector.tensor_tensor(w_lo[n][:, cols], weight_banks[bank][:], w_hi[n][:, cols].bitcast(F32),
                                            ALU.subtract).then_inc(w_lo_ready, 1)

            weights(0)
            dve.wait_ge(bqk_bank_ready, 1)
            nc.vector.tensor_copy(bqk[:], jobp[0][:, 0:2 * NPAIR]).then_inc(bqk_ready, 1)
            weights(1)
            for s in AHEAD:
                job(before, s)
                if JOBS[s][0] == "xt":
                    weights(2)
                    dve.wait_ge(sim_loaded, 32)
                    nc.vector.tensor_scalar(temp_c[:], temp_b[:], CLAMP_MAX, None, ALU.min).then_inc(temp_ready, 1)
                if JOBS[s][0] == "k":
                    dve.wait_ge(bv_loaded, 16)
                    link(nc.vector.tensor_scalar(bv8[:], bv_b[:], INV_SCALE, None, ALU.mult))
            dve.wait_ge(small_loaded, 16 * n_small)
            up = small_in[:, 2, 0:RSUM]
            nc.vector.tensor_copy(up_parts[:, 0, 0:RSUM], up)
            link(nc.vector.tensor_copy(up_parts[:, 1, 0:RSUM], up))
            nc.vector.tensor_tensor(up_parts[:, 2, 0:RSUM], up, up_parts[:, 0, 0:RSUM].bitcast(F32), ALU.subtract)\
                .then_inc(up_ready, 1)
            link(nc.vector.tensor_tensor(sim_sq[:], sim_b[:], sim_b[:], ALU.mult))
            nc.vector.tensor_reduce(sim_norm[:, 0, :], sim_sq[:].rearrange("p a b -> p b a"), AX_X, ALU.add)\
                .then_inc(simsq_ready, 1)

            def rest():
                dve.wait_ge(small_bank_ready, 1)
                link(nc.vector.tensor_copy(wt_hi[:], zp[:, 0:P]))
                nc.vector.tensor_tensor(wt_lo[:], zp[:, 0:P], wt_hi[:].bitcast(F32), ALU.subtract).then_inc(small_ready, 1)
                nc.vector.tensor_copy(wrd[:], zp[:, P:P + NRD]).then_inc(small_ready, 1)
                nc.vector.tensor_copy(wut[:], zp[0:PARTS * PART, 2 * P:3 * P]).then_inc(small_ready, 1)
                dve.wait_ge(simnorm_ready, 1)
                link(nc.vector.tensor_scalar(sim_norm[:, 2, :], sim_norm[:, 1, :], L2_EPS, None, ALU.max))
                link(nc.vector.reciprocal(sim_norm[:, 3, :], sim_norm[:, 2, :]))
                link(nc.vector.tensor_tensor(sim_unit[:], sim_b[:].rearrange("p a b -> p b a"),
                                             sim_norm[:, 3, :].unsqueeze(2).to_broadcast([P, NEXP, PROJ]), ALU.mult))
                dve.wait_ge(gate_scale_ready, 1)
                nc.vector.tensor_scalar(simn[:], sim_unit[:], gate_scale[:, 0:1], None, ALU.mult).then_inc(simn_ready, 1)

            def reciprocals(c, s):
                dve.wait_ge(p_ready, c.head(s, 1))
                nc.vector.reciprocal(rden[:, s % NROT, :], den[:, s % NROT, :]).then_inc(r_ready, 1)

            def maximum(c, s):
                cols = width(s)
                for h in range(2):
                    scored, read = c.fixed(c.head(s, h)), c.fixed(c.head(s - 2, h))
                    dve.wait_ge(consts_ready, 3)
                    dve.wait_ge(s_ready, scored)
                    wait(dve, p_ready, read)
                    nc.vector.tensor_tensor_reduce(
                        out=sm[:, s % 2, h, 0:cols], in0=scores[h][:, 0:cols], in1=mask[:, S - cols:S],
                        scale=-INV_SCALE, scalar=HUGE, op0=ALU.add, op1=ALU.min,
                        accum_out=nmax[:, s % NROT, h:h + 1]).then_inc(sm_ready, 1)

            def evacuate_pt(c, s):
                dve.wait_ge(t_ready, c.head(s, 1))
                i, p = s % NBLK, s // NBLK
                if i == 0:
                    wait(dve, pv_ready, c.values(p - 2, 1))
                src = ptp[1][:, 0:width(s)].rearrange("p (j q) -> p j q", q=P)
                nc.vector.tensor_copy(pt[:, p % 2, 1, 0:i + 1, P * i:P * i + P], src).then_inc(pt_ready[1], 1)

            def low_z(c, p, h):
                dve.wait_ge(z_hi_ready, c.values(p, h))
                high, half, low = z_views(p, h)
                nc.vector.tensor_tensor(low, half, high.bitcast(F32), ALU.subtract).then_inc(z_ready, 1)

            def final(c):
                dve.wait_ge(y_ready, c.at(1, 0))
                dve.wait_ge(xres_loaded, c.at(16, 0))
                nc.vector.tensor_tensor(osb[:].rearrange("p n e -> p (n e)"), jobp[bank_of(STEP_OUT)][:],
                                        xres[:].rearrange("p n e -> p (n e)"), ALU.add).then_inc(final_ready, 1)

            def router(c, t):
                def prior(n):
                    dve.wait_ge(r_chain, c.at(R_CHAIN, n))

                def over_experts(m):
                    return m.unsqueeze(2).to_broadcast([P, NBLK, NEXP])

                t -= R_FIRST
                logits, shifted, exps, weights, chosen, routed = (lg[:, n, :, :] for n in (1, 2, 3, 4, 5, 6))
                taken = row[:, 4, :]
                if t == 0:
                    dve.wait_ge(products_ready, c.at(1, 1))
                    nc.vector.tensor_reduce(unorm[:, 0, :], usq[:], AX_X, ALU.add).then_inc(unorm_ready, 1)
                    nc.vector.tensor_reduce(lg[:, 0, :, :], uprod[:], AX_X, ALU.add).then_inc(r_chain, 1)
                if t == 4:
                    dve.wait_ge(unorm_root, c.at(1, 1))
                    nc.vector.tensor_scalar(unorm[:, 2, :], unorm[:, 1, :], L2_EPS, None, ALU.max).then_inc(r_chain, 1)
                if t == 5:
                    prior(2)
                    nc.vector.reciprocal(unorm[:, 3, :], unorm[:, 2, :]).then_inc(r_chain, 1)
                if t == 6:
                    prior(3)
                    nc.vector.tensor_tensor(logits, lg[:, 0, :, :], over_experts(unorm[:, 3, :]), ALU.mult)\
                        .then_inc(r_chain, 1)
                if t == 7:
                    prior(4)
                    nc.vector.tensor_reduce(row[:, 0, :], logits, AX_X, ALU.max).then_inc(r_chain, 1)
                if t == 8:
                    prior(5)
                    nc.vector.tensor_tensor(shifted, logits, over_experts(row[:, 0, :]), ALU.subtract)\
                        .then_inc(lg_ready, 1)
                if t == 13:
                    dve.wait_ge(lg_exp, c.at(1, 1))
                    nc.vector.tensor_reduce(row[:, 1, :], exps, AX_X, ALU.add).then_inc(r_chain, 1)
                if t == 14:
                    prior(6)
                    nc.vector.reciprocal(row[:, 2, :], row[:, 1, :]).then_inc(r_chain, 1)
                if t == 15:
                    prior(7)
                    nc.vector.tensor_tensor(weights, exps, over_experts(row[:, 2, :]), ALU.mult).then_inc(r_chain, 1)
                if t == 16:
                    prior(8)
                    nc.vector.tensor_reduce(row[:, 3, :], weights, AX_X, ALU.max).then_inc(r_chain, 1)
                if t == 17:
                    prior(9)
                    nc.vector.tensor_tensor(chosen, weights, over_experts(row[:, 3, :]), ALU.is_ge)\
                        .then_inc(r_chain, 1)
                if t == 18:
                    prior(10)
                    nc.vector.tensor_copy(taken, lg[:, 5, :, 0]).then_inc(r_chain, 1)
                for e in range(1, NEXP):
                    if t == 17 + 2 * e:
                        prior(9 + 2 * e)
                        nc.vector.tensor_tensor(lg[:, 5, :, e], lg[:, 5, :, e], taken, ALU.is_gt).then_inc(r_chain, 1)
                    if t == 18 + 2 * e:
                        prior(10 + 2 * e)
                        nc.vector.tensor_tensor(taken, taken, lg[:, 5, :, e], ALU.max).then_inc(r_chain, 1)
                if t == 25:
                    prior(17)
                    nc.vector.tensor_tensor(routed, weights, chosen, ALU.mult).then_inc(r_chain, 1)
                if t == 26:
                    prior(18)
                    r0 = 0
                    for e, r in enumerate(RANKS):
                        last = nc.vector.tensor_tensor(gated[:, :, r0:r0 + r], dn[:, :, r0:r0 + r],
                                                       lg[:, 6, :, e:e + 1].to_broadcast([P, NBLK, r]), ALU.mult)
                        r0 += r
                    last.then_inc(r_chain, 1)
                if t == 27:
                    prior(19)
                    nc.vector.tensor_copy(gated_parts[:, :, 0, 0:RSUM], gated[:])
                    nc.vector.tensor_copy(gated_parts[:, :, 2, 0:RSUM], gated[:]).then_inc(r_chain, 1)
                if t == 28:
                    prior(20)
                    nc.vector.tensor_tensor(gated_parts[:, :, 1, 0:RSUM], gated[:],
                                            gated_parts[:, :, 0, 0:RSUM].bitcast(F32), ALU.subtract)\
                        .then_inc(gated_ready, 1)

            def step(c, s, first=False, last=False, tail=False):
                if not tail:
                    maximum(c, s)
                    router(c, 2 * s)
                unit = due(s, 1, 1, first, tail)
                if unit is not None:
                    reciprocals(c, unit)
                unit = due(s, LAG_T, 1, first, tail)
                if unit is not None:
                    evacuate_pt(c, unit)
                for h in range(2):
                    p = due(s, LAG_Z[h], NBLK, first, tail)
                    if p is not None:
                        low_z(c, p, h)
                if s == STEP_FINAL and not first:
                    final(c)
                if tail:
                    return
                if s > 0 and s - 1 in JOBS and not (last and s - 1 in AHEAD):
                    job(c, s - 1)
                if s == 0 and not first:
                    job(c, UNITS - 1, back=1)
                if s in STEPS_STATS and not last:
                    statistics(c, STEPS_STATS.index(s))
                if s == STEP_AGGR and not last:
                    aggregates(c)
                if s == STEP_VAR and not last:
                    variances(c)
                router(c, 2 * s + 1)

            def batch(b, first, last):
                c = Counts(dve, b)
                for s in range(UNITS):
                    step(c, s, first, last)
                    if first and s == 1:
                        rest()

            batch(0, True, False)
            with dve.Fori(1, NBATCH - 1) as b:
                batch(b, False, False)
            batch(NBATCH - 1, False, True)
            c = Counts(dve, NBATCH)
            for s in range(STEP_FINAL + 1):
                step(c, s, tail=True)

        @block.tensor
        def _(pe):
            def job(c, s):
                kind, n = JOBS[s]
                bank = bank_of(s)
                dst = jobp[bank]
                if s == STEP_OUT + 2:
                    wait(pe, final_ready, c.at(1, 0))
                wait(pe, job_done[bank], c.job(s) - 1)
                if kind in ("q", "k"):
                    w = 0 if kind == "q" else 1
                    cols = slice(P * n, P * n + P)
                    for a, m in ((w_hi, xt_hi), (w_hi, xt_lo), (w_lo, xt_hi)):
                        tokens = m[:].rearrange("p (i q t) -> p i t q", q=P // 2, t=2) if kind == "q" else m[:]
                        done = nc.tensor.matmul(dst[:], a[w][:, cols], tokens, start=a is w_hi and m is xt_hi,
                                                stop=a is w_lo)
                elif kind == "v":
                    cols, keys = slice(S * (n // NBLK), S * (n // NBLK) + S), slice(P * (n % NBLK), P * (n % NBLK) + P)
                    for a, m in ((xt_hi, w_hi), (xt_hi, w_lo), (xt_lo, w_hi)):
                        done = nc.tensor.matmul(dst[:], a[:, keys], m[2][:, cols], start=a is xt_hi and m is w_hi,
                                                stop=a is xt_lo)
                elif kind == "xt":
                    pe.wait_ge(xn_ready, c.at(1, 2))
                    for i in range(NBLK):
                        done = nc.tensor.transpose(dst[:, P * i:P * i + P], xn[:, i, :], ident[:])
                elif kind == "router":
                    pe.wait_ge(small_ready, 3)
                    for i in range(NBLK):
                        done = nc.tensor.matmul(dst[:, RPAD * i:RPAD * i + NRD], xt[:, P * i:P * i + P], wrd[:],
                                                start=True, stop=True)
                else:
                    pe.wait_ge(gated_ready, c.at(1, 1))
                    for i in range(NBLK):
                        done = nc.tensor.transpose(dst[0:PARTS * PART, P * i:P * i + P],
                                                   gated_parts[:, i, :, :].rearrange("p a b -> p (a b)").bitcast(F32),
                                                   ident[:])
                done.then_inc(job_ready[bank], 1)

            def weights(n):
                pe.wait_ge(w_loaded[n], 16)
                for bank in (2 * n, 2 * n + 1):
                    for j in range(4):
                        last = nc.tensor.transpose(weight_banks[bank][:, P * j:P * j + P],
                                                   w_in[n][:, 4 * (bank % 2) + j, :], ident[:])
                    last.then_inc(wbank_ready, 1)

            pe.wait_ge(consts_ready, 1)
            weights(0)
            pe.wait_ge(bqk_loaded, 32)
            nc.tensor.transpose(jobp[0][:, 0:2 * NPAIR], bqk_in[:], ident[0:2 * NPAIR, 0:2 * NPAIR])\
                .then_inc(bqk_bank_ready, 1)
            weights(1)
            for s in AHEAD:
                kind = JOBS[s][0]
                if kind == "q":
                    pe.wait_ge(w_lo_ready, 2)
                if kind == "k":
                    pe.wait_ge(w_lo_ready, 4)
                    pe.wait_ge(bqk_ready, 1)
                if kind == "v":
                    pe.wait_ge(w_lo_ready, 6)
                job(Counts(pe, -1), s)
                if kind == "xt":
                    weights(2)

            def rest():
                pe.wait_ge(small_loaded, 16 * n_small)
                nc.tensor.transpose(zp[:, 0:P], small_in[:, 0, :], ident[:])
                nc.tensor.transpose(zp[:, P:P + NRD], small_in[0:NRD, 1, :], ident[0:NRD, 0:NRD])
                pe.wait_ge(up_ready, 1)
                nc.tensor.transpose(zp[0:PARTS * PART, 2 * P:3 * P],
                                    up_parts[:].rearrange("p a b -> p (a b)").bitcast(F32), ident[:])\
                    .then_inc(small_bank_ready, 1)

            def score(c, s):
                i, p = s % NBLK, s // NBLK
                if i == 0:
                    for ahead in LEAD.values():
                        js = (s - ahead) % UNITS
                        pe.wait_ge(job_done[bank_of(js)], c.job(js, back=int(s < ahead)))
                    pe.wait_ge(k_copied, c.at(64 * NPAIR, 64 * (p + 1)))
                queries = slice(P * i, P * i + P)
                for h in range(2):
                    wait(pe, sm_ready, c.head(s - 1, h))
                    nc.tensor.matmul(scores[h][:, 0:width(s)], q_parts[:, h, p % 2, queries],
                                     k_twice[:, h, p % 2, 0:width(s)], start=True, stop=False)
                for h in range(2):
                    nc.tensor.matmul(scores[h][:, 0:width(s)], q_parts[own(h), h, p % 2, queries],
                                     k_lo[own(h), p % 2, 0:width(s)], start=False, stop=True).then_inc(s_ready, 1)

            def transpose(c, s):
                for h in range(2):
                    pe.wait_ge(pn_ready, c.head(s, h))
                    wait(pe, pt_ready[h], c.unit(s - 1))
                    for j in range(s % NBLK + 1):
                        done = nc.tensor.transpose(ptp[h][:, P * j:P * j + P], prob[:, s % NROT, h, P * j:P * j + P],
                                                   ident[:])
                    done.then_inc(t_ready, 1)

            def values(c, p, h):
                pe.wait_ge(pt_ready[h], c.unit(NBLK * p + NBLK - 1))
                wait(pe, z_ready, c.values(p, h) - 1)
                if h == 0 and p in (0, NPAIR // 2):
                    for bank in range(2):
                        made = [js for js in V_STEPS[:4] if js not in AHEAD] if p == 0 else V_STEPS[4:]
                        made = [js for js in made if bank_of(js) == bank]
                        if made:
                            pe.wait_ge(job_done[bank], c.job(max(made)))
                col = DH * (2 * (p % NPAIR) + h)
                z0 = S // 2 * h
                for j in reversed(range(NBLK)):
                    for odd in range(2):
                        seen = pt[:, p % 2, h, j, :].rearrange("p (i t q) -> p i t q", t=2, q=P // 2)[:, j:, odd, :]
                        done = nc.tensor.matmul(zp[DH * odd:DH * odd + DH, z0 + P // 2 * j:z0 + S // 2],
                                                v_sb[:, j, col:col + DH], seen, start=j == NBLK - 1, stop=j == 0,
                                                skip_group_check=True)
                done.then_inc(pv_ready, 1)

            def project(c, o, quarter):
                pe.wait_ge(z_ready, c.values(OCT_PAIRS * (o + 1) - 1, 1))
                pe.wait_ge(proj_split, 2)
                cols = OCT * ROWS * (o % NOCT)
                for n in range(NPAIR // 4 * quarter, NPAIR // 4 * (quarter + 1)):
                    for a, m in ((proj_hi, z_hi), (proj_hi, z_lo), (proj_lo, z_hi)):
                        done = nc.tensor.matmul(outp[:, cols:cols + OCT * ROWS], a[:, n, :], m[:, o % 2, n, :, :],
                                                start=False, stop=False, skip_group_check=True)
                if quarter == 3:
                    done.then_inc(o_ready, 1)

            def base(c):
                wait(pe, y_copied, c.at(1, 0))
                for a, m in ((wt_hi, xt_hi), (wt_hi, xt_lo), (wt_lo, xt_hi)):
                    nc.tensor.matmul(outp[:], a[:], m[:], start=a is wt_hi and m is xt_hi, stop=False,
                                     skip_group_check=True)

            def lora(c):
                pe.wait_ge(job_done[bank_of(STEP_GATED)], c.job(STEP_GATED))
                nc.tensor.matmul(outp[:], wut[:], gated_t[:], start=False, stop=False, skip_group_check=True)

            def transpose_sum(c, tail):
                bank = bank_of(STEP_OUT)
                if not tail:
                    pe.wait_ge(job_done[bank], c.job(STEP_OUT))
                pe.wait_ge(y_copied, c.at(1, 0))
                for i in range(NBLK):
                    cols = slice(P * i, P * i + P)
                    done = nc.tensor.transpose(jobp[bank][:, cols], y_t[:, cols], ident[:])
                done.then_inc(y_ready, 1)

            def step(c, s, first=False, last=False, tail=False):
                if not tail:
                    score(c, s)
                unit = due(s, LAG_T, 1, first, tail)
                if unit is not None:
                    transpose(c, unit)
                for h in range(2):
                    p = due(s, LAG_PV[h], NBLK, first, tail)
                    if p is not None:
                        values(c, p, h)
                for o in range(NOCT):
                    for quarter in range(4):
                        n = due(s, OCT_STEPS * o + LAG_OUT[o][quarter], UNITS, first, tail)
                        if n is not None:
                            project(c, NOCT * n + o, quarter)
                if s == STEP_OUT and not first:
                    transpose_sum(c, tail)
                if tail:
                    return
                if s == STEP_BASE:
                    base(c)
                if s == STEP_LORA:
                    lora(c)
                if s in JOBS and not (last and s in AHEAD):
                    job(c, s)

            def batch(b, first, last):
                c = Counts(pe, b)
                for s in range(UNITS):
                    step(c, s, first, last)
                    if first and s == 0:
                        rest()

            batch(0, True, False)
            with pe.Fori(1, NBATCH - 1) as b:
                batch(b, False, False)
            batch(NBATCH - 1, False, True)
            c = Counts(pe, NBATCH)
            for s in range(STEP_OUT + 1):
                step(c, s, tail=True)


_INS = ["x", "Wq", "bq", "Wk", "bk", "Wv", "bv", "proj"]
_FFN = ["W", "Wp", "bp", "sim", "temp"]
_NAMES = ([f"L0_attn_{n}" for n in _INS] + [f"L0_ffn_{n}" for n in _FFN]
          + [f"L0_ffn_Wd{n}" for n in range(NEXP)] + [f"L0_ffn_Wu{n}" for n in range(NEXP)])


def kernel(**inputs):
    import numpy as _np
    import concourse.bacc as _bacc
    from concourse import mybir as _mybir
    from concourse.bass_utils import run_bass_kernel_spmd as _run

    nc = _bacc.Bacc("TRN2", target_bir_lowering=False, num_devices=1)
    arrays, args = {}, []
    for name in _NAMES:
        a = _np.ascontiguousarray(inputs[name])
        arrays[f"in_{name}_dram"] = a
        args.append(nc.dram_tensor(f"in_{name}_dram", a.shape, _mybir.dt.from_np(a.dtype), kind="ExternalInput").ap())
    out = nc.dram_tensor("out_0_dram", (NBATCH, S, E), F32, kind="ExternalOutput").ap()
    build(nc, *args[:13], args[13:17], args[17:21], out)
    r = _run(nc, [arrays], core_ids=[0])
    return r.results[0]["out_0_dram"]
```
